# Optimizing a Trainium2 kernel written in Bass

```python
import numpy as np
import jax
import jax.numpy as jnp

def _softmax(x, axis=-1):
    return jax.nn.softmax(x, axis=axis)

def _gelu(x):
    return jax.nn.gelu(x, approximate=True)

def _silu(x):
    return jax.nn.silu(x)

def _sigmoid(x):
    return jax.nn.sigmoid(x)

def _layernorm(x, axis=-1, eps=1e-05):
    m = jnp.mean(x, axis=axis, keepdims=True)
    v = jnp.var(x, axis=axis, keepdims=True)
    return (x - m) / jnp.sqrt(v + eps)

def _scatter_add(tgt, idx, src, axis=0):
    return tgt.at[idx].add(src)

def _segment_sum(src, seg, n):
    return jax.ops.segment_sum(src, seg, n)
kernel_name = 'mk_sandwich_d1_jaxref_r4_4ece8e'

def setup_inputs(seed: int=0):
    np.random.seed(seed)
    _w = jnp.asarray

    def _L0_attn_setup():
        import jax, jax.numpy as jnp
        import numpy as np
        from jax import lax
        D_MODEL, D_STATE, D_CONV, EXPAND, HEADDIM = (256, 128, 4, 2, 64)
        D_INNER = EXPAND * D_MODEL
        NHEADS = D_INNER // HEADDIM
        CONV_DIM = D_INNER + 2 * D_STATE
        D_IN_PROJ = 2 * D_INNER + 2 * D_STATE + NHEADS

        def _mamba2(x, in_proj_w, conv_w, conv_b, dt_bias, A_log, D, norm_w, out_proj_w):
            b, l, _ = x.shape
            zxbcdt = x @ in_proj_w.T
            z = zxbcdt[..., :D_INNER]
            xBC = zxbcdt[..., D_INNER:D_INNER + CONV_DIM]
            dt = zxbcdt[..., D_INNER + CONV_DIM:]
            xBC_pad = jnp.pad(xBC, ((0, 0), (D_CONV - 1, 0), (0, 0)))
            windows = jnp.stack([xBC_pad[:, k:k + l, :] for k in range(D_CONV)], axis=-1)
            xBC = jax.nn.silu(jnp.einsum('blck,ck->blc', windows, conv_w) + conv_b)
            xs = xBC[..., :D_INNER]
            B = xBC[..., D_INNER:D_INNER + D_STATE]
            C = xBC[..., D_INNER + D_STATE:]
            xh = xs.reshape(b, l, NHEADS, HEADDIM)
            dt = jax.nn.softplus(dt + dt_bias)
            A = -jnp.exp(A_log)
            dA = jnp.exp(dt * A)
            xdt = xh * dt[..., None]

            def step(S, inp):
                dA_t, xdt_t, B_t, C_t = inp
                S = dA_t[:, :, None, None] * S + xdt_t[..., None] * B_t[:, None, None, :]
                y_t = jnp.einsum('bhpn,bn->bhp', S, C_t)
                return (S, y_t)
            S0 = jnp.zeros((b, NHEADS, HEADDIM, D_STATE), x.dtype)
            _, y = lax.scan(step, S0, (dA.transpose(1, 0, 2), xdt.transpose(1, 0, 2, 3), B.transpose(1, 0, 2), C.transpose(1, 0, 2)))
            y = y.transpose(1, 0, 2, 3) + D[None, None, :, None] * xh
            y = y.reshape(b, l, D_INNER)
            y = y * jax.nn.silu(z)
            y = y * lax.rsqrt(jnp.mean(y * y, axis=-1, keepdims=True) + 1e-05) * norm_w
            return y @ out_proj_w.T
        key = jax.random.key(seed)
        ks = jax.random.split(key, 9)
        b, l = (2, 512)
        x = jax.random.normal(ks[0], (b, l, D_MODEL), jnp.float32)
        in_proj_w = jax.random.normal(ks[1], (D_IN_PROJ, D_MODEL), jnp.float32) * 0.02
        conv_w = jax.random.normal(ks[2], (CONV_DIM, D_CONV), jnp.float32) * 0.2
        conv_b = jax.random.normal(ks[3], (CONV_DIM,), jnp.float32) * 0.02
        dt_bias = jnp.log(jnp.expm1(jax.random.uniform(ks[4], (NHEADS,), jnp.float32, 0.001, 0.1)))
        A_log = jnp.log(jax.random.uniform(ks[5], (NHEADS,), jnp.float32, 1.0, 16.0))
        D = jax.random.normal(ks[6], (NHEADS,), jnp.float32)
        norm_w = jnp.ones((D_INNER,), jnp.float32)
        out_proj_w = jax.random.normal(ks[7], (D_MODEL, D_INNER), jnp.float32) * 0.02
        return {'x': x, 'in_proj_w': in_proj_w, 'conv_w': conv_w, 'conv_b': conv_b, 'dt_bias': dt_bias, 'A_log': A_log, 'D': D, 'norm_w': norm_w, 'out_proj_w': out_proj_w}
    _L0_attn_in = _L0_attn_setup()

    def _L0_ffn_setup():
        import jax, jax.numpy as jnp
        import numpy as np
        EMB = 256
        FF = 4 * EMB

        def _ternary(w):
            scale = jnp.maximum(jnp.mean(jnp.abs(w)), 1e-08)
            w_t = jnp.clip(jnp.round(w / scale), -1.0, 1.0)
            return w + jax.lax.stop_gradient(w_t - w)
        key = jax.random.key(seed)
        kx, k1, k2, kb1, kb2 = jax.random.split(key, 5)
        x = jax.random.normal(kx, (4, 512, EMB), dtype=jnp.float32)
        lim1 = 1.0 / np.sqrt(EMB)
        lim2 = 1.0 / np.sqrt(FF)
        W1 = jax.random.uniform(k1, (FF, EMB), jnp.float32, -lim1, lim1)
        b1 = jax.random.uniform(kb1, (FF,), jnp.float32, -lim1, lim1)
        W2 = jax.random.uniform(k2, (EMB, FF), jnp.float32, -lim2, lim2)
        b2 = jax.random.uniform(kb2, (EMB,), jnp.float32, -lim2, lim2)
        return {'x': x, 'W1': W1, 'b1': b1, 'W2': W2, 'b2': b2}
    _L0_ffn_in = _L0_ffn_setup()
    _d = {'L0_attn_x': _L0_attn_in['x'], 'L0_attn_in_proj_w': _L0_attn_in['in_proj_w'], 'L0_attn_conv_w': _L0_attn_in['conv_w'], 'L0_attn_conv_b': _L0_attn_in['conv_b'], 'L0_attn_dt_bias': _L0_attn_in['dt_bias'], 'L0_attn_A_log': _L0_attn_in['A_log'], 'L0_attn_D': _L0_attn_in['D'], 'L0_attn_norm_w': _L0_attn_in['norm_w'], 'L0_attn_out_proj_w': _L0_attn_in['out_proj_w'], 'L0_ffn_W1': _L0_ffn_in['W1'], 'L0_ffn_b1': _L0_ffn_in['b1'], 'L0_ffn_W2': _L0_ffn_in['W2'], 'L0_ffn_b2': _L0_ffn_in['b2']}
    _x0 = _d['L0_attn_x']
    _d['L0_attn_x'] = jax.random.normal(jax.random.fold_in(jax.random.key(seed), 1), (16, 512, 256), dtype=_x0.dtype)
    del _x0
    return _d

def reference(L0_attn_x, L0_attn_in_proj_w, L0_attn_conv_w, L0_attn_conv_b, L0_attn_dt_bias, L0_attn_A_log, L0_attn_D, L0_attn_norm_w, L0_attn_out_proj_w, L0_ffn_W1, L0_ffn_b1, L0_ffn_W2, L0_ffn_b2):

    def _L0_attn_ref(x, in_proj_w, conv_w, conv_b, dt_bias, A_log, D, norm_w, out_proj_w):
        import jax, jax.numpy as jnp
        import numpy as np
        from jax import lax
        D_MODEL, D_STATE, D_CONV, EXPAND, HEADDIM = (256, 128, 4, 2, 64)
        D_INNER = EXPAND * D_MODEL
        NHEADS = D_INNER // HEADDIM
        CONV_DIM = D_INNER + 2 * D_STATE
        D_IN_PROJ = 2 * D_INNER + 2 * D_STATE + NHEADS

        def _mamba2(x, in_proj_w, conv_w, conv_b, dt_bias, A_log, D, norm_w, out_proj_w):
            b, l, _ = x.shape
            zxbcdt = x @ in_proj_w.T
            z = zxbcdt[..., :D_INNER]
            xBC = zxbcdt[..., D_INNER:D_INNER + CONV_DIM]
            dt = zxbcdt[..., D_INNER + CONV_DIM:]
            xBC_pad = jnp.pad(xBC, ((0, 0), (D_CONV - 1, 0), (0, 0)))
            windows = jnp.stack([xBC_pad[:, k:k + l, :] for k in range(D_CONV)], axis=-1)
            xBC = jax.nn.silu(jnp.einsum('blck,ck->blc', windows, conv_w) + conv_b)
            xs = xBC[..., :D_INNER]
            B = xBC[..., D_INNER:D_INNER + D_STATE]
            C = xBC[..., D_INNER + D_STATE:]
            xh = xs.reshape(b, l, NHEADS, HEADDIM)
            dt = jax.nn.softplus(dt + dt_bias)
            A = -jnp.exp(A_log)
            dA = jnp.exp(dt * A)
            xdt = xh * dt[..., None]

            def step(S, inp):
                dA_t, xdt_t, B_t, C_t = inp
                S = dA_t[:, :, None, None] * S + xdt_t[..., None] * B_t[:, None, None, :]
                y_t = jnp.einsum('bhpn,bn->bhp', S, C_t)
                return (S, y_t)
            S0 = jnp.zeros((b, NHEADS, HEADDIM, D_STATE), x.dtype)
            _, y = lax.scan(step, S0, (dA.transpose(1, 0, 2), xdt.transpose(1, 0, 2, 3), B.transpose(1, 0, 2), C.transpose(1, 0, 2)))
            y = y.transpose(1, 0, 2, 3) + D[None, None, :, None] * xh
            y = y.reshape(b, l, D_INNER)
            y = y * jax.nn.silu(z)
            y = y * lax.rsqrt(jnp.mean(y * y, axis=-1, keepdims=True) + 1e-05) * norm_w
            return y @ out_proj_w.T
        return x + _mamba2(x, in_proj_w, conv_w, conv_b, dt_bias, A_log, D, norm_w, out_proj_w)

    def _L0_ffn_ref(x, W1, b1, W2, b2):
        import jax, jax.numpy as jnp
        import numpy as np
        EMB = 256
        FF = 4 * EMB

        def _ternary(w):
            scale = jnp.maximum(jnp.mean(jnp.abs(w)), 1e-08)
            w_t = jnp.clip(jnp.round(w / scale), -1.0, 1.0)
            return w + jax.lax.stop_gradient(w_t - w)
        h = jnp.einsum('bsd,fd->bsf', x, _ternary(W1)) + b1
        h = jax.nn.gelu(h, approximate=False)
        out = jnp.einsum('bsf,df->bsd', h, _ternary(W2)) + b2
        return out
    x = L0_attn_x
    x = x + _layernorm(_L0_attn_ref(_layernorm(x, axis=-1), L0_attn_in_proj_w, L0_attn_conv_w, L0_attn_conv_b, L0_attn_dt_bias, L0_attn_A_log, L0_attn_D, L0_attn_norm_w, L0_attn_out_proj_w), axis=-1)
    x = x + _layernorm(_L0_ffn_ref(_layernorm(x, axis=-1), L0_ffn_W1, L0_ffn_b1, L0_ffn_W2, L0_ffn_b2), axis=-1)
    return x

_drawn_inputs = setup_inputs


def setup_inputs(seed=0):
    import zlib

    import numpy as np

    out = dict(_drawn_inputs(seed))
    spreads = {'L0_attn_norm_w': (1.0, 0.2)}
    factors = {}
    for name, (base, spread) in spreads.items():
        noise = np.random.default_rng([zlib.crc32(name.encode()), seed]).standard_normal(out[name].shape)
        drawn = base * np.exp(spread * noise) if base else spread * noise
        out[name] = jnp.asarray(drawn.astype(out[name].dtype))
    for name, factor in factors.items():
        out[name] = (out[name] * factor).astype(out[name].dtype)
    return out
```

```python
from contextlib import ExitStack

import numpy as np
import concourse.bass as bass
from concourse import mybir

F32 = mybir.dt.float32
F32R = mybir.dt.float32r
ALU = mybir.AluOpType
ACT = mybir.ActivationFunctionType
AX = mybir.AxisListType

P = 128
CONSTS = 13
SP_STEPS = 15
CARRY = 4
EPS = 1e-5

STEP = [
    ("A", "norm", 0),
    ("S", "front", 0), ("F", "up", 0), ("A", "uT", 0), ("F", "up", 1),
    ("S", "inter", 0), ("A", "dt", 0), ("A", "conv", 0),
    ("S", "intra", 0), ("A", "silu", 0), ("A", "dtT", 0), ("F", "up", 2), ("F", "up", 3),
    ("S", "gateT", 0), ("A", "cum", 0), ("S", "project", 0), ("A", "conv", 1),
    ("S", "state", 0), ("S", "residual", 0), ("A", "cumT", 0), ("A", "silu", 1),
    ("S", "front", 1), ("A", "z", 0), ("F", "down", 0),
    ("S", "norm2", 0), ("S", "inter", 1), ("A", "conv", 2),
    ("S", "intra", 1), ("A", "silu", 2), ("A", "z", 1), ("F", "down", 1),
    ("S", "gateT", 1), ("S", "project", 1), ("S", "state", 1),
    ("S", "residual", 1), ("S", "norm2", 1),
]


def build(nc, x, w_in, conv_w, conv_b, dt_bias, a_log, d_skip, norm_w, w_out, w1, b1, w2, b2,
          cum_dram, out):
    B, L, DM = x.shape
    KM = DM // P
    DIN = w_in.shape[1]
    DI = w_out.shape[0]
    KI = DI // P
    NH = dt_bias.shape[0]
    HD = DI // NH
    CH = conv_w.shape[1]
    TAPS = conv_w.shape[2]
    XS = KI
    FF = w1.shape[1]
    KF = FF // P
    HALF = L // 2
    J = HALF // P
    UW = CARRY + HALF
    assert (KM, KI, CH, J, KF, TAPS, L // HALF) == (2, 4, 6, 2, 8, 4, 2)

    xv = x.rearrange("b (s j p) d -> b s p j d", s=2, p=P)
    ov = out.rearrange("b (s j p) d -> b s j p d", s=2, p=P)

    with ExitStack() as ctx:
        def sb(name, shape, dt=F32):
            return ctx.enter_context(nc.sbuf_tensor(name, shape, dt))

        def bank(name):
            return ctx.enter_context(nc.psum_tensor(name, [P, 512], F32))

        def sem(name):
            return ctx.enter_context(nc.semaphore(name))

        win_f = sb("win_f", [P, KM, DIN])
        win_hi = sb("win_hi", [P, KM, DIN], F32R)
        win_lo = sb("win_lo", [P, KM, DIN], F32R)
        wdt = sb("wdt", [P, KM, P], F32R)
        wout_hi = sb("wout_hi", [P, KI, DM], F32R)
        wout_lo = sb("wout_lo", [P, KI, DM], F32R)
        w1_t = sb("w1_t", [P, KM * FF], F32R)
        w2_t = sb("w2_t", [P, KF * DM], F32R)
        convw = sb("convw", [P, CH, TAPS])
        convb = sb("convb", [P, CH])
        b1s = sb("b1s", [P, KF])
        nws = sb("nws", [P, KI])
        b2s = sb("b2s", [P, DM])
        dtb = sb("dtb", [P, NH])
        a_neg = sb("a_neg", [P, NH])
        dsk = sb("dsk", [P, NH])
        ident = sb("ident", [P, P])
        upper = sb("upper", [P, P])
        lower = sb("lower", [P, P])
        ones = sb("ones", [P, P])
        mhalf = sb("mhalf", [P, J])
        absum = sb("absum", [P, 2])
        thr = sb("thr", [P, 2])
        nthr = sb("nthr", [P, 2])
        X = [sb(f"X{s}", [P, J, DM]) for s in range(2)]
        U = [sb(f"U{s}", [P, J, DM]) for s in range(2)]
        st1 = sb("st1", [P, J, 6])
        mv1 = sb("mv1", [P, J, 2])
        ve1 = sb("ve1", [P, J])
        rs1 = sb("rs1", [P, J])
        uTh = [sb(f"uTh{s}", [P, KM, UW], F32R) for s in range(2)]
        uTl = [sb(f"uTl{s}", [P, KM, UW], F32R) for s in range(2)]
        acc = [sb(f"acc{q}", [P, 2, HALF]) for q in range(2)]
        xbc = [sb(f"xbc{s}", [P, CH, HALF]) for s in range(2)]
        sz = [sb(f"sz{s}", [P, J, DI]) for s in range(2)]
        dtr = sb("dtr", [P, HALF])
        dtt = sb("dtt", [P, J, 2 * NH])
        sp = sb("sp", [P, 8, J, NH])
        dts = [sb(f"dts{s}", [P, J, NH]) for s in range(2)]
        dA = sb("dA", [P, J, NH])
        cum = [sb(f"cum{s}", [P, J, NH]) for s in range(2)]
        ecum = [sb(f"ecum{s}", [P, 3, J, NH]) for s in range(2)]
        dtdec = [sb(f"dtdec{s}", [P, J, NH]) for s in range(2)]
        cumr = sb("cumr", [J * NH, P])
        R = [sb(f"R{s}", [P, J, NH, P]) for s in range(2)]
        xtok = [sb(f"xtok{j}", [P, DI]) for j in range(J)]
        bg = [sb(f"bg{j}", [P, 2, P]) for j in range(J)]
        gm = [sb(f"gm{j}", [P, P]) for j in range(J)]
        xdt = [sb(f"xdt{j}", [P, DI]) for j in range(J)]
        xst = [sb(f"xst{j}", [P, DI]) for j in range(J)]
        xd = [sb(f"xd{j}", [P, DI]) for j in range(J)]
        t1 = [sb(f"t1{j}", [P, DI]) for j in range(J)]
        g = [sb(f"g{j}", [P, DI]) for j in range(J)]
        S = sb("S", [P, DI])
        sqj = sb("sqj", [P, DI])
        ss = sb("ss", [P, J])
        vg = sb("vg", [P, J])
        rg = sb("rg", [P, J])
        gTh = [sb(f"gTh{j}", [P, KI, P], F32R) for j in range(J)]
        gTl = [sb(f"gTl{j}", [P, KI, P], F32R) for j in range(J)]
        r = [sb(f"r{j}", [P, DM]) for j in range(J)]
        sta = sb("sta", [P, J, 6])
        mva = sb("mva", [P, J, 2])
        vea = sb("vea", [P, J])
        rsa = sb("rsa", [P, J])
        x1 = [sb(f"x1{s}", [P, J, DM]) for s in range(2)]
        st2 = sb("st2", [P, J, 6])
        mv2 = sb("mv2", [P, J, 2])
        ve2 = sb("ve2", [P, J])
        rs2 = sb("rs2", [P, J])
        u2 = [sb(f"u2{j}", [P, DM]) for j in range(J)]
        u2Th = [sb(f"u2Th{s}", [P, KM, HALF], F32R) for s in range(2)]
        u2Tl = [sb(f"u2Tl{s}", [P, KM, HALF], F32R) for s in range(2)]
        hf = [sb(f"hf{q}", [P, 2, HALF]) for q in range(2)]
        hh = sb("hh", [P, KF, HALF], F32R)
        hl = sb("hl", [P, KF, HALF], F32R)
        ffo = [sb(f"ffo{j}", [P, DM]) for j in range(J)]
        stf = sb("stf", [P, J, 6])
        mvf = sb("mvf", [P, J, 2])
        vef = sb("vef", [P, J])
        rsf = sb("rsf", [P, J])
        ob = [sb(f"ob{j}", [P, DM]) for j in range(J)]

        wout_f = xbc[0][:].rearrange("p c t -> p (c t)")[:, 0:KI * DM].rearrange("p (c n) -> p c n", c=KI)
        w1_f = R[0][:].rearrange("p j h i -> p (j h i)")
        w2_f = R[1][:].rearrange("p j h i -> p (j h i)")

        pA = [bank(f"pA{i}") for i in range(2)]
        pT = bank("pT")
        pG = bank("pG")
        pY = bank("pY")
        pS = bank("pS")
        pF = [bank(f"pF{i}") for i in range(2)]

        w_ld = {n: sem(f"{n}_ld") for n in ("win", "wout", "w1", "w2", "small")}
        x_ld = [sem(f"x_ld{s}") for s in range(2)]
        cum_st = sem("cum_st")
        r_ld = [sem(f"r_ld{s}") for s in range(2)]
        out_st = [sem(f"out_st{j}") for j in range(J)]
        consts = sem("consts")
        prep = sem("prep")
        absum_ready = sem("absum_ready")
        absum_ps = sem("absum_ps")
        weights_ready = sem("weights_ready")
        a_exp = sem("a_exp")
        ln1_mv = sem("ln1_mv")
        ln1_ve = sem("ln1_ve")
        ln1_rstd = sem("ln1_rstd")
        u_ready = sem("u_ready")
        uT_ps = sem("uT_ps")
        uTh_ready = sem("uTh_ready")
        uTl_ready = sem("uTl_ready")
        dt_ps = sem("dt_ps")
        dtr_ready = sem("dtr_ready")
        conv_ps = sem("conv_ps")
        conv_first = sem("conv_first")
        conv_tap = sem("conv_tap")
        conv_done = sem("conv_done")
        xbc_ready = sem("xbc_ready")
        dtT_ps = sem("dtT_ps")
        dtt_ready = sem("dtt_ready")
        sp_step = sem("sp_step")
        sp_exp = sem("sp_exp")
        dA_ready = sem("dA_ready")
        cum_ps = sem("cum_ps")
        cum_ready = sem("cum_ready")
        ecum_ready = sem("ecum_ready")
        dtdec_ready = sem("dtdec_ready")
        cumT_ps = sem("cumT_ps")
        cumr_ready = sem("cumr_ready")
        z_ps = sem("z_ps")
        sz_ready = sem("sz_ready")
        xT_ps = sem("xT_ps")
        g_ps = sem("g_ps")
        xtok_ready = sem("xtok_ready")
        bg_ready = sem("bg_ready")
        gm_ready = sem("gm_ready")
        xdt_ready = sem("xdt_ready")
        xst_ready = sem("xst_ready")
        xd_ready = sem("xd_ready")
        diff_ready = sem("diff_ready")
        exp_ready = sem("exp_ready")
        mix_ready = sem("mix_ready")
        inter_ps = sem("inter_ps")
        t1_ready = sem("t1_ready")
        yx_ready = sem("yx_ready")
        intra_ps = sem("intra_ps")
        y_ready = sem("y_ready")
        g_ready = sem("g_ready")
        ss_ready = sem("ss_ready")
        vg_ready = sem("vg_ready")
        rg_ready = sem("rg_ready")
        gT_ps = sem("gT_ps")
        gTh_ready = sem("gTh_ready")
        gTl_ready = sem("gTl_ready")
        proj_ps = sem("proj_ps")
        r_ready = sem("r_ready")
        state_ps = sem("state_ps")
        s_scaled = sem("s_scaled")
        s_ready = sem("s_ready")
        lna_mv = sem("lna_mv")
        lna_ve = sem("lna_ve")
        lna_rstd = sem("lna_rstd")
        rn_ready = sem("rn_ready")
        x1_ready = sem("x1_ready")
        ln2_mv = sem("ln2_mv")
        ln2_ve = sem("ln2_ve")
        ln2_rstd = sem("ln2_rstd")
        u2_ready = sem("u2_ready")
        u2T_ps = sem("u2T_ps")
        u2Th_ready = sem("u2Th_ready")
        u2Tl_ready = sem("u2Tl_ready")
        up_ps = sem("up_ps")
        gelu_ready = sem("gelu_ready")
        hh_ready = sem("hh_ready")
        hl_ready = sem("hl_ready")
        down_ps = sem("down_ps")
        ffo_ready = sem("ffo_ready")
        lnf_mv = sem("lnf_mv")
        lnf_ve = sem("lnf_ve")
        lnf_rstd = sem("lnf_rstd")
        fn_ready = sem("fn_ready")
        ob_ready = sem("ob_ready")

        def passed(k, n, i):
            return k[0] * (2 * n) + (k[1] * n + i + 1)

        def need(eng, s, count):
            if not isinstance(count, int) or count > 0:
                eng.wait_ge(s, count)

        def back(k, n):
            h = k[1] - n
            return (k[0] + h // 2, h % 2)

        def first_tile(k, j):
            return (k[1], j) == (0, 0)

        def last_tile(k, j):
            return (k[1], j) == (1, J - 1)

        def inter_count(k, j):
            return 3 * k[0] + 2 * k[1] + j

        def state_count(k, j):
            return 3 * k[0] + 2 * k[1] + j + 1

        def run(eng, units):
            def step(a, s, f):
                for stage, unit, arg in STEP:
                    k = {"A": a, "S": s, "F": f}[stage]
                    if k is not None and (stage, unit) in units:
                        units[stage, unit](k, arg)

            def sequence(b, first=False, last=False):
                step((b, 1), (b, 0), None if first else (b + -1, 1))
                step(None if last else (b + 1, 0), (b, 1), (b, 0))

            step((0, 0), None, None)
            sequence(0, first=True)
            with eng.Fori(1, B - 1) as b:
                sequence(b)
            sequence(B - 1, last=True)
            step(None, None, (B - 1, 1))

        block = ctx.enter_context(nc.Block())

        @block.sync
        def _(sy):
            sy.dma_start(win_f[:], w_in.rearrange("(c p) n -> p c n", p=P)).then_inc(w_ld["win"], 16)
            sy.dma_start(X[0][:], xv[0, 0]).then_inc(x_ld[0], 16)
            sy.dma_start(convw[:], conv_w).then_inc(w_ld["small"], 16)
            sy.dma_start(convb[:], conv_b).then_inc(w_ld["small"], 16)
            sy.dma_start(b1s[:], b1).then_inc(w_ld["small"], 16)
            sy.dma_start(nws[:], norm_w).then_inc(w_ld["small"], 16)
            for dst, src in ((b2s, b2), (dtb, dt_bias), (a_neg, a_log), (dsk, d_skip)):
                sy.dma_start(dst[:], src.partition_broadcast(P)).then_inc(w_ld["small"], 16)
            sy.dma_start(X[1][:], xv[0, 1]).then_inc(x_ld[1], 16)
            sy.dma_start(wout_f, w_out.rearrange("(c p) n -> p c n", p=P)).then_inc(w_ld["wout"], 16)
            sy.dma_start(w1_f.rearrange("p (c n) -> p c n", c=KM),
                         w1.rearrange("(c p) n -> p c n", p=P)).then_inc(w_ld["w1"], 16)
            sy.dma_start(w2_f.rearrange("p (c n) -> p c n", c=KF),
                         w2.rearrange("(c p) n -> p c n", p=P)).then_inc(w_ld["w2"], 16)

            def cum_out_and_back(k, _):
                need(sy, cumr_ready, passed(k, 1, 0))
                sy.dma_start(cum_dram[k[1]], cumr[:]).then_inc(cum_st, 16)
                sy.wait_ge(cum_st, passed(k, 16, 15))
                need(sy, intra_ps, passed(back(k, 2), J, J - 1))
                sy.dma_start(R[k[1]][:].rearrange("p j h i -> p (j h i)"),
                             cum_dram[k[1]].rearrange("a i -> (a i)").partition_broadcast(P)
                             ).then_inc(r_ld[k[1]], 16)

            def load_next_x(k, j):
                if j == J - 1 and not (isinstance(k[0], int) and k[0] == B - 1):
                    need(sy, x1_ready, passed(k, J, J - 1))
                    sy.dma_start(X[k[1]][:], xv[k[0] + 1, k[1]]).then_inc(x_ld[k[1]], 16)

            def store(k, j):
                need(sy, ob_ready, passed(k, J, j))
                sy.dma_start(ov[k[0], k[1], j], ob[j][:]).then_inc(out_st[j], 16)

            run(sy, {("A", "cumT"): cum_out_and_back, ("S", "residual"): load_next_x,
                     ("F", "down"): store})
            for j in range(J):
                sy.wait_ge(out_st[j], 16 * 2 * B)

        @block.gpsimd
        def _(pool):
            nc.gpsimd.memset(ident[:], 0.0).then_inc(consts, 1)
            nc.gpsimd.memset(upper[:], 1.0).then_inc(consts, 1)
            nc.gpsimd.memset(lower[:], 1.0).then_inc(consts, 1)
            nc.gpsimd.memset(ones[:], 1.0).then_inc(consts, 1)
            nc.gpsimd.memset(mhalf[:], -0.5).then_inc(consts, 1)
            for s in range(2):
                nc.gpsimd.memset(uTh[s][:, :, 0:CARRY].bitcast(F32), 0.0).then_inc(consts, 1)
                nc.gpsimd.memset(uTl[s][:, :, 0:CARRY].bitcast(F32), 0.0).then_inc(consts, 1)
            nc.gpsimd.memset(wdt[:].bitcast(F32), 0.0).then_inc(consts, 1)
            pool.wait_ge(consts, 5)
            nc.gpsimd.affine_select(out=ident[:], in_=ident[:], compare_op=ALU.not_equal, fill=1.0,
                                    base=0, pattern=[[-1, P]], channel_multiplier=1).then_inc(consts, 1)
            nc.gpsimd.affine_select(out=upper[:], in_=upper[:], compare_op=ALU.is_ge, fill=0.0,
                                    base=0, pattern=[[1, P]], channel_multiplier=-1).then_inc(consts, 1)

            nc.gpsimd.affine_select(out=lower[:], in_=lower[:], compare_op=ALU.is_ge, fill=0.0,
                                    base=-1, pattern=[[-1, P]], channel_multiplier=1).then_inc(consts, 1)
            pool.wait_ge(consts, CONSTS)

            def rstd(ve_ready, rstd_ready, ve, rs, k, n, i, cols):
                need(pool, ve_ready, passed(k, n, i))
                nc.gpsimd.tensor_tensor(rs[:, cols], ve[:, cols], mhalf[:, 0:cols.stop - cols.start],
                                        ALU.pow).then_inc(rstd_ready, 1)

            def ln1(k, _):
                need(pool, u_ready, passed(back(k, 1), J, J - 1))
                rstd(ln1_ve, ln1_rstd, ve1, rs1, k, 1, 0, slice(0, J))

            def front(k, j):
                b, s = k
                tile = passed(k, J, j)
                before = passed(back(k, 1), J, j)
                need(pool, bg_ready, tile)
                need(pool, mix_ready, before)
                nc.gpsimd.tensor_tensor(gm[j][:], bg[j][:, 1, :], upper[:], ALU.mult).then_inc(gm_ready, 1)
                need(pool, xtok_ready, tile)
                need(pool, dtdec_ready, passed(k, 1, 0))
                heads = xtok[j][:].rearrange("p (h d) -> p h d", h=NH)
                if not last_tile(k, j):
                    need(pool, state_ps, 3 * b + (-1 if (s, j) == (0, 1) else s))
                    nc.gpsimd.tensor_tensor(xst[j][:].rearrange("p (h d) -> p h d", h=NH), heads,
                                            dtdec[s][:, j, :].unsqueeze(2).to_broadcast([P, NH, HD]),
                                            ALU.mult).then_inc(xst_ready, 1)
                need(pool, y_ready, before)
                nc.gpsimd.tensor_tensor(xd[j][:].rearrange("p (h d) -> p h d", h=NH), heads,
                                        dsk[:].unsqueeze(2).to_broadcast([P, NH, HD]),
                                        ALU.mult).then_inc(xd_ready, 1)
                need(pool, exp_ready, tile)
                pool.wait_ge(gm_ready, tile)
                nc.gpsimd.tensor_tensor(R[s][:, j], R[s][:, j],
                                        gm[j][:].unsqueeze(1).to_broadcast([P, NH, P]),
                                        ALU.mult).then_inc(mix_ready, 1)

            def inter(k, j):
                if not first_tile(k, j):
                    need(pool, t1_ready, inter_count(k, j))
                    pool.wait_ge(xd_ready, passed(k, J, j))
                    nc.gpsimd.tensor_tensor(xd[j][:], t1[j][:], xd[j][:], ALU.add).then_inc(yx_ready, 1)

            def gate(k, j):
                rstd(vg_ready, rg_ready, vg, rg, k, J, j, slice(j, j + 1))

            def residual(k, j):
                rstd(lna_ve, lna_rstd, vea, rsa, k, J, j, slice(j, j + 1))
                need(pool, rn_ready, passed(k, J, j))
                need(pool, ob_ready, passed(back(k, 2), J, j))
                nc.gpsimd.tensor_tensor(x1[k[1]][:, j], X[k[1]][:, j], r[j][:], ALU.add).then_inc(x1_ready, 1)

            def norm2(k, j):
                rstd(ln2_ve, ln2_rstd, ve2, rs2, k, J, j, slice(j, j + 1))

            def up(k, q):
                need(pool, hh_ready, passed(k, 4, q))
                nc.gpsimd.tensor_tensor(hl[:, 2 * q:2 * q + 2, :], hf[q % 2][:],
                                        hh[:, 2 * q:2 * q + 2, :].bitcast(F32),
                                        ALU.subtract).then_inc(hl_ready, 1)

            def down(k, j):
                rstd(lnf_ve, lnf_rstd, vef, rsf, k, J, j, slice(j, j + 1))
                need(pool, fn_ready, passed(k, J, j))
                need(pool, out_st[j], passed(back(k, 1), 16, 15))
                nc.gpsimd.tensor_tensor(ob[j][:], x1[k[1]][:, j], ffo[j][:], ALU.add).then_inc(ob_ready, 1)

            run(pool, {("A", "norm"): ln1, ("S", "front"): front, ("S", "inter"): inter,
                       ("S", "gateT"): gate, ("S", "residual"): residual, ("S", "norm2"): norm2,
                       ("F", "up"): up, ("F", "down"): down})

        @block.vector
        def _(dve):
            dve.wait_ge(w_ld["win"], 16)
            nc.vector.tensor_copy(win_hi[:], win_f[:]).then_inc(prep, 1)
            dve.wait_ge(prep, 1)
            nc.vector.tensor_tensor(win_lo[:], win_f[:], win_hi[:].bitcast(F32), ALU.subtract).then_inc(prep, 1)
            dve.wait_ge(prep, 2)
            dve.wait_ge(consts, CONSTS)
            nc.vector.tensor_copy(wdt[:, :, 0:NH], win_hi[:, :, DIN - NH:DIN].bitcast(F32)).then_inc(prep, 1)
            nc.vector.tensor_copy(wdt[:, :, NH:2 * NH], win_lo[:, :, DIN - NH:DIN].bitcast(F32)).then_inc(prep, 1)
            dve.wait_ge(a_exp, 1)
            nc.vector.tensor_scalar(a_neg[:], a_neg[:], -1.0, None, ALU.mult).then_inc(prep, 1)
            dve.wait_ge(w_ld["wout"], 16)
            for c in range(KI):
                nc.vector.tensor_scalar(wout_f[:, c, :], wout_f[:, c, :], nws[:, c:c + 1], None,
                                        ALU.mult).then_inc(prep, 1)
            dve.wait_ge(prep, 5 + KI)
            nc.vector.tensor_copy(wout_hi[:], wout_f).then_inc(prep, 1)
            dve.wait_ge(prep, 6 + KI)
            nc.vector.tensor_tensor(wout_lo[:], wout_f, wout_hi[:].bitcast(F32), ALU.subtract).then_inc(prep, 1)
            for n, (name, wf) in enumerate((("w1", w1_f), ("w2", w2_f))):
                dve.wait_ge(w_ld[name], 16)
                nc.vector.tensor_reduce(absum[:, n:n + 1], wf, axis=AX.X, op=ALU.add,
                                        apply_absolute_value=True).then_inc(absum_ready, 1)
            dve.wait_ge(absum_ps, 1)
            nc.vector.tensor_scalar(thr[:], pG[:, 0:2], 1.0 / (DM * FF), 1e-8, ALU.mult, ALU.max).then_inc(prep, 1)
            dve.wait_ge(prep, 8 + KI)
            nc.vector.tensor_scalar(nthr[:], thr[:], -0.5, None, ALU.mult).then_inc(prep, 1)
            nc.vector.tensor_scalar(thr[:], thr[:], 0.5, None, ALU.mult).then_inc(prep, 1)
            dve.wait_ge(prep, 10 + KI)
            for n, (wf, wt) in enumerate(((w1_f, w1_t), (w2_f, w2_t))):
                nc.vector.tensor_scalar(wt[:], wf, nthr[:, n:n + 1], 1.0, ALU.is_ge,
                                        ALU.subtract).then_inc(prep, 1)
                dve.wait_ge(prep, 11 + KI + 2 * n)
                nc.vector.scalar_tensor_tensor(wt[:], wf, thr[:, n:n + 1], wt[:].bitcast(F32), ALU.is_gt,
                                               ALU.add).then_inc(prep, 1)
            dve.wait_ge(prep, 14 + KI)
            nc.vector.memset(sp[:], 0.0).then_inc(weights_ready, 1)
            dve.wait_ge(weights_ready, 1)

            def norm_tail(st, mv, ve, s_mv, s_ve, k, j):
                dve.drain()
                nc.vector.bn_aggr(mv[:, j, :], st[:, j, :]).then_inc(s_mv, 1)
                dve.wait_ge(s_mv, passed(k, J, j))
                nc.vector.tensor_scalar(ve[:, j:j + 1], mv[:, j, 1:2], EPS, None, ALU.add).then_inc(s_ve, 1)

            def normalize(dst, src, mv, rs, j, done):
                nc.vector.tensor_scalar(dst, src, mv[:, j, 0:1], rs[:, j:j + 1], ALU.subtract,
                                        ALU.mult).then_inc(done, 1)

            def by_head(ap):
                return ap.rearrange("p (h d) -> p h d", h=NH)

            def per_head(ap):
                return ap.unsqueeze(2).to_broadcast([P, NH, HD])

            def ln1(k, _):
                dve.wait_ge(x_ld[k[1]], 16 * (k[0] + 1))
                for j in range(J):
                    nc.vector.bn_stats(st1[:, j, :], X[k[1]][:, j, :])
                for j in range(J):
                    if j == 0:
                        dve.drain()
                    nc.vector.bn_aggr(mv1[:, j, :], st1[:, j, :]).then_inc(ln1_mv, 1)
                dve.wait_ge(ln1_mv, passed(k, J, J - 1))
                nc.vector.tensor_scalar(ve1[:], mv1[:, :, 1], EPS, None, ALU.add).then_inc(ln1_ve, 1)

            def u_and_lo(k, _):
                s = k[1]
                need(dve, ln1_rstd, passed(k, 1, 0))
                for j in range(J):
                    normalize(U[s][:, j, :], X[s][:, j, :], mv1, rs1, j, u_ready)
                need(dve, uTh_ready, passed(k, 1, 0))
                if s == 1:
                    need(dve, uTl_ready, passed(back(k, 1), 1, 0))
                    nc.vector.tensor_copy(uTl[1][:, :, 0:CARRY], uTl[0][:, :, UW - CARRY:UW].bitcast(F32))
                nc.vector.tensor_tensor(uTl[s][:, :, CARRY:UW],
                                        pA[0][:].rearrange("p (c t) -> p c t", c=KM),
                                        uTh[s][:, :, CARRY:UW].bitcast(F32),
                                        ALU.subtract).then_inc(uTl_ready, 1)

            def conv(k, q):
                for tap in range(1, TAPS):
                    for c in range(2):
                        m = 2 * q + c
                        if tap == 1:
                            need(dve, conv_first, passed(k, CH, m))
                        else:
                            dve.wait_ge(conv_tap, passed(k, 2 * CH, 4 * q + 2 * (tap - 2) + c))
                        w = TAPS - 1 - tap
                        nc.vector.scalar_tensor_tensor(
                            acc[q % 2][:, c, :], pA[c][:, 1 + w:1 + w + HALF], convw[:, m, w:w + 1],
                            acc[q % 2][:, c, :], ALU.mult, ALU.add
                        ).then_inc(conv_done if tap == TAPS - 1 else conv_tap, 1)

            def sp_did(k, i):
                dve.wait_ge(sp_step, passed(k, SP_STEPS, i))

            def softplus_front(k, _):
                v, a = sp[:, 0], sp[:, 1]
                need(dve, dtt_ready, passed(k, 1, 0))
                nc.vector.tensor_tensor(v, dtt[:, :, 0:NH], dtt[:, :, NH:2 * NH], ALU.add).then_inc(sp_step, 1)
                sp_did(k, 0)
                nc.vector.tensor_tensor(v, v, dtb[:].unsqueeze(1).to_broadcast([P, J, NH]), ALU.add).then_inc(sp_step, 1)
                sp_did(k, 1)
                nc.vector.scalar_tensor_tensor(a, v, -1.0, v, ALU.mult, ALU.max).then_inc(sp_step, 1)

            def softplus_back(k, _):
                v, e, d, rc, z, qq, p = (sp[:, n] for n in (0, 2, 3, 4, 5, 6, 7))
                need(dve, sp_exp, passed(k, 1, 0))
                nc.vector.tensor_scalar(d, e, 2.0, None, ALU.add).then_inc(sp_step, 1)
                sp_did(k, 3)
                nc.vector.reciprocal(rc, d).then_inc(sp_step, 1)
                sp_did(k, 4)
                nc.vector.tensor_tensor(z, e, rc, ALU.mult).then_inc(sp_step, 1)
                sp_did(k, 5)
                nc.vector.tensor_tensor(qq, z, z, ALU.mult).then_inc(sp_step, 1)
                sp_did(k, 6)
                nc.vector.tensor_scalar(p, qq, 1.0 / 11, None, ALU.mult).then_inc(sp_step, 1)
                for n, odd in enumerate((9, 7, 5, 3)):
                    sp_did(k, 7 + n)
                    nc.vector.scalar_tensor_tensor(p, p, 1.0 / odd, qq, ALU.add, ALU.mult).then_inc(sp_step, 1)
                sp_did(k, 11)
                nc.vector.scalar_tensor_tensor(p, p, 1.0, z, ALU.add, ALU.mult).then_inc(sp_step, 1)
                nc.vector.tensor_scalar(d, v, 0.0, None, ALU.max).then_inc(sp_step, 1)
                sp_did(k, 13)
                nc.vector.scalar_tensor_tensor(dts[k[1]][:], p, 2.0, d, ALU.mult, ALU.add).then_inc(sp_step, 1)
                sp_did(k, 14)
                nc.vector.tensor_tensor(dA[:], dts[k[1]][:], a_neg[:].unsqueeze(1).to_broadcast([P, J, NH]),
                                        ALU.mult).then_inc(dA_ready, 1)

            def dt_decay(k, _):
                need(dve, ecum_ready, passed(k, 1, 0))
                nc.vector.tensor_tensor(dtdec[k[1]][:], dts[k[1]][:], ecum[k[1]][:, 2], ALU.mult).then_inc(dtdec_ready, 1)

            def front(k, j):
                s = k[1]
                dve.wait_ge(r_ld[s], 16 * (k[0] + 1))
                need(dve, cum_ready, passed(k, 1, 0))
                for h in range(NH):
                    last = nc.vector.tensor_scalar(R[s][:, j, h, :], R[s][:, j, h, :], cum[s][:, j, h:h + 1], 0.0,
                                                   ALU.subtract, ALU.min)
                last.then_inc(diff_ready, 1)
                need(dve, xtok_ready, passed(k, J, j))
                need(dve, intra_ps, passed(back(k, 1), J, j))
                nc.vector.tensor_tensor(by_head(xdt[j][:]), by_head(xtok[j][:]), per_head(dts[s][:, j, :]),
                                        ALU.mult).then_inc(xdt_ready, 1)

            def inter(k, j):
                if not first_tile(k, j):
                    need(dve, inter_ps, inter_count(k, j))
                    nc.vector.tensor_tensor(by_head(t1[j][:]), by_head(pY[:]), per_head(ecum[k[1]][:, 0, j, :]),
                                            ALU.mult).then_inc(t1_ready, 1)

            def gate(k, j):
                need(dve, intra_ps, passed(k, J, j))
                if first_tile(k, j):
                    need(dve, xd_ready, passed(k, J, j))
                else:
                    need(dve, yx_ready, inter_count(k, j))
                nc.vector.tensor_tensor(t1[j][:], pY[:], xd[j][:], ALU.add).then_inc(y_ready, 1)
                dve.wait_ge(y_ready, passed(k, J, j))
                need(dve, sz_ready, passed(k, J, j))
                nc.vector.tensor_tensor(g[j][:], t1[j][:], sz[k[1]][:, j, :], ALU.mult).then_inc(g_ready, 1)

            def gate_lo(k, j):
                need(dve, ss_ready, passed(k, J, j))
                nc.vector.tensor_scalar(vg[:, j:j + 1], ss[:, j:j + 1], 1.0 / DI, EPS, ALU.mult, ALU.add).then_inc(vg_ready, 1)
                need(dve, gTh_ready, passed(k, J, j))
                nc.vector.tensor_tensor(gTl[j][:], pT[:].rearrange("p (c t) -> p c t", c=KI), gTh[j][:].bitcast(F32),
                                        ALU.subtract).then_inc(gTl_ready, 1)

            def project(k, j):
                need(dve, proj_ps, passed(k, J, j))
                need(dve, rg_ready, passed(k, J, j))
                nc.vector.scalar_tensor_tensor(r[j][:], pY[:, 0:DM], rg[:, j:j + 1], U[k[1]][:, j, :], ALU.mult,
                                               ALU.add).then_inc(r_ready, 1)

            def state(k, j):
                b, s = k
                if last_tile(k, j):
                    return
                need(dve, inter_ps, inter_count(k, j))
                if not first_tile(k, j):
                    nc.vector.tensor_tensor(by_head(S[:]), by_head(S[:]), per_head(ecum[s][:, 1, j, :]),
                                            ALU.mult).then_inc(s_scaled, 1)
                    dve.wait_ge(s_scaled, 2 * b + 2 * s + j)
                need(dve, state_ps, state_count(k, j))
                if first_tile(k, j):
                    nc.vector.tensor_copy(S[:], pS[:]).then_inc(s_ready, 1)
                else:
                    nc.vector.tensor_tensor(S[:], pS[:], S[:], ALU.add).then_inc(s_ready, 1)

            def residual(k, j):
                dve.wait_ge(r_ready, passed(k, J, j))
                nc.vector.bn_stats(sta[:, j, :], r[j][:])
                norm_tail(sta, mva, vea, lna_mv, lna_ve, k, j)
                need(dve, lna_rstd, passed(k, J, j))
                normalize(r[j][:], r[j][:], mva, rsa, j, rn_ready)

            def norm2(k, j):
                need(dve, x1_ready, passed(k, J, j))
                nc.vector.bn_stats(st2[:, j, :], x1[k[1]][:, j, :])
                norm_tail(st2, mv2, ve2, ln2_mv, ln2_ve, k, j)
                need(dve, ln2_rstd, passed(k, J, j))
                normalize(u2[j][:], x1[k[1]][:, j, :], mv2, rs2, j, u2_ready)
                need(dve, u2Th_ready, passed(k, J, j))
                cols = slice(j * P, (j + 1) * P)
                nc.vector.tensor_tensor(u2Tl[k[1]][:, :, cols], pT[:, 0:DM].rearrange("p (c t) -> p c t", c=KM),
                                        u2Th[k[1]][:, :, cols].bitcast(F32), ALU.subtract).then_inc(u2Tl_ready, 1)

            def down(k, j):
                need(dve, down_ps, passed(k, J, j))
                need(dve, ob_ready, passed(back(k, 1), J, j))
                nc.vector.tensor_tensor(ffo[j][:], pF[j][:, 0:DM], b2s[:], ALU.add).then_inc(ffo_ready, 1)
                dve.wait_ge(ffo_ready, passed(k, J, j))
                nc.vector.bn_stats(stf[:, j, :], ffo[j][:])
                norm_tail(stf, mvf, vef, lnf_mv, lnf_ve, k, j)
                need(dve, lnf_rstd, passed(k, J, j))
                normalize(ffo[j][:], ffo[j][:], mvf, rsf, j, fn_ready)

            run(dve, {("A", "norm"): ln1, ("A", "uT"): u_and_lo, ("A", "conv"): conv,
                      ("A", "dtT"): softplus_front, ("A", "cum"): softplus_back, ("A", "cumT"): dt_decay,
                      ("S", "front"): front, ("S", "inter"): inter, ("S", "intra"): gate,
                      ("S", "gateT"): gate_lo, ("S", "project"): project, ("S", "state"): state,
                      ("S", "residual"): residual, ("S", "norm2"): norm2, ("F", "down"): down})

        @block.scalar
        def _(act):
            act.wait_ge(w_ld["small"], 16 * 8)
            nc.scalar.activation(a_neg[:], a_neg[:], ACT.Exp).then_inc(a_exp, 1)
            act.wait_ge(consts, CONSTS)

            def uT_hi(k, _):
                s = k[1]
                need(act, uT_ps, passed(k, 1, 0))
                need(act, z_ps, passed(back(k, 2), J, J - 1))
                if s == 1:
                    need(act, uTh_ready, passed(back(k, 1), 1, 0))
                    nc.scalar.copy(uTh[1][:, :, 0:CARRY], uTh[0][:, :, UW - CARRY:UW].bitcast(F32))
                nc.scalar.copy(uTh[s][:, :, CARRY:UW],
                               pA[0][:].rearrange("p (c t) -> p c t", c=KM)).then_inc(uTh_ready, 1)

            def dt_out(k, _):
                need(act, dt_ps, passed(k, 1, 0))
                need(act, dtT_ps, passed(back(k, 1), 1, 0))
                nc.scalar.copy(dtr[:], pA[1][:, 0:HALF]).then_inc(dtr_ready, 1)

            def conv_first_tap(k, q):
                need(act, xbc_ready, passed(k, 3, 0) if q == 2 else passed(back(k, 1), 3, 2 if q == 0 else 1))
                for c in range(2):
                    m = 2 * q + c
                    need(act, conv_ps, passed(k, CH, m))
                    nc.scalar.activation(acc[q % 2][:, c, :], pA[c][:, CARRY:UW], ACT.Identity,
                                         bias=convb[:, m:m + 1], scale=convw[:, m, TAPS - 1:TAPS]).then_inc(conv_first, 1)

            def silu(k, q):
                need(act, conv_done, passed(k, CH, 2 * q + 1))
                need(act, intra_ps, passed(back(k, 2), J, J - 1))
                nc.scalar.activation(xbc[k[1]][:, 2 * q:2 * q + 2, :], acc[q % 2][:], ACT.Silu).then_inc(xbc_ready, 1)

            def softplus_exp(k, _):
                need(act, dtT_ps, passed(k, 1, 0))
                need(act, sp_step, passed(back(k, 1), SP_STEPS, 0))
                nc.scalar.copy(dtt[:], pA[0][:, 0:J * P].rearrange("p (j n) -> p j n", j=J)[:, :, 0:2 * NH]).then_inc(dtt_ready, 1)
                need(act, sp_step, passed(k, SP_STEPS, 2))
                nc.scalar.activation(sp[:, 2], sp[:, 1], ACT.Exp, scale=-1.0).then_inc(sp_exp, 1)

            def cum_out(k, _):
                n = J * NH
                need(act, cum_ps, passed(k, 1, 0))
                nc.scalar.copy(cum[k[1]][:].rearrange("p j h -> p (j h)"), pA[1][:, 0:n]).then_inc(cum_ready, 1)
                nc.scalar.activation(ecum[k[1]][:].rearrange("p a j h -> p (a j h)"), pA[1][:, 0:3 * n],
                                     ACT.Exp).then_inc(ecum_ready, 1)

            def cumT_out(k, _):
                need(act, cumT_ps, passed(k, 1, 0))
                need(act, cum_st, passed(back(k, 1), 16, 15))
                nc.scalar.copy(cumr[:], pA[0][0:J * NH, 0:P]).then_inc(cumr_ready, 1)

            def z_silu(k, j):
                need(act, z_ps, passed(k, J, j))
                need(act, g_ready, passed(back(k, 2), J, j))
                nc.scalar.activation(sz[k[1]][:, j, :], pA[1 - j][:], ACT.Silu).then_inc(sz_ready, 1)

            def front(k, j):
                s = k[1]
                before = passed(back(k, 1), J, j)
                need(act, xT_ps, passed(k, J, j))
                need(act, xdt_ready, before)
                need(act, xd_ready, before)
                nc.scalar.copy(xtok[j][:], pT[:]).then_inc(xtok_ready, 1)
                need(act, g_ps, passed(k, J, j))
                need(act, gm_ready, before)
                need(act, state_ps, 3 * k[0] + (-1 if (s, j) == (0, 1) else s + j))
                nc.scalar.copy(bg[j][:].rearrange("p a t -> p (a t)"), pG[:, 0:2 * P]).then_inc(bg_ready, 1)
                need(act, diff_ready, passed(k, J, j))
                nc.scalar.activation(R[s][:, j], R[s][:, j], ACT.Exp).then_inc(exp_ready, 1)

            def gate_hi(k, j):
                need(act, g_ready, passed(k, J, j))
                need(act, ss_ready, passed(back((k[0], k[1]), 1) if j == 0 else k, J, 1 if j == 0 else 0))
                nc.scalar.activation(sqj[:], g[j][:], ACT.Square, accum_out=ss[:, j:j + 1]).then_inc(ss_ready, 1)
                need(act, gT_ps, passed(k, J, j))
                need(act, proj_ps, passed(back(k, 1), J, j))
                nc.scalar.copy(gTh[j][:], pT[:].rearrange("p (c t) -> p c t", c=KI)).then_inc(gTh_ready, 1)

            def u2_hi(k, j):
                need(act, u2T_ps, passed(k, J, j))
                need(act, up_ps, passed(back(k, 2), 4, 3))
                nc.scalar.copy(u2Th[k[1]][:, :, j * P:(j + 1) * P],
                               pT[:, 0:DM].rearrange("p (c t) -> p c t", c=KM)).then_inc(u2Th_ready, 1)

            def up(k, q):
                need(act, up_ps, passed(k, 4, q))
                need(act, hl_ready, passed(k if q >= 2 else back(k, 1), 4, (q + 2) % 4))
                for c in range(2):
                    nc.scalar.activation(hf[q % 2][:, c, :], pF[q % 2][:, c * HALF:(c + 1) * HALF], ACT.Gelu,
                                         bias=b1s[:, 2 * q + c:2 * q + c + 1]).then_inc(gelu_ready, 1)
                act.wait_ge(gelu_ready, passed(k, KF, 2 * q + 1))
                need(act, down_ps, passed(back(k, 1), J, J - 1))
                nc.scalar.copy(hh[:, 2 * q:2 * q + 2, :], hf[q % 2][:]).then_inc(hh_ready, 1)

            run(act, {("A", "uT"): uT_hi, ("A", "dt"): dt_out, ("A", "conv"): conv_first_tap, ("A", "silu"): silu,
                      ("A", "dtT"): softplus_exp, ("A", "cum"): cum_out, ("A", "cumT"): cumT_out, ("A", "z"): z_silu,
                      ("S", "front"): front, ("S", "gateT"): gate_hi, ("S", "norm2"): u2_hi, ("F", "up"): up})

        @block.tensor
        def _(pe):
            pe.wait_ge(absum_ready, 2)
            pe.wait_ge(consts, CONSTS)
            nc.tensor.matmul(pG[:, 0:2], ones[:], absum[:], start=True, stop=True).then_inc(absum_ps, 1)
            pe.wait_ge(weights_ready, 1)

            def transpose(dst, src):
                return nc.tensor.matmul(dst, src, ident[:], is_transpose=True, start=True, stop=True)

            def uT(k, _):
                s = k[1]
                need(pe, u_ready, passed(k, J, J - 1))
                need(pe, sz_ready, passed(back(k, 1), J, 1))
                for c in range(KM):
                    for j in range(J):
                        last = transpose(pA[0][:, c * HALF + j * P:c * HALF + (j + 1) * P], U[s][:, j, c * P:(c + 1) * P])
                last.then_inc(uT_ps, 1)

            def dt(k, _):
                s = k[1]
                need(pe, uTl_ready, passed(k, 1, 0))
                need(pe, conv_done, passed(back(k, 1), CH, 5))
                for c in range(KM):
                    for n, uT_part in enumerate((uTh, uTl)):
                        last = nc.tensor.matmul(pA[1][:, 0:HALF], wdt[:, c, :], uT_part[s][:, c, CARRY:UW],
                                                start=(c, n) == (0, 0), stop=(c, n) == (KM - 1, 1))
                last.then_inc(dt_ps, 1)

            def conv_in(k, q):
                s = k[1]
                for i in range(2):
                    m = 2 * q + i
                    if q == 0:
                        need(pe, (uTl_ready, dtr_ready)[i], passed(k, 1, 0))
                    elif q == 1:
                        need(pe, (dtt_ready, ecum_ready)[i], passed(k, 1, 0))
                    elif i == 0:
                        need(pe, cumr_ready, passed(k, 1, 0))
                    else:
                        need(pe, sz_ready, passed(k, J, 0))
                    cols = slice(DI + m * P, DI + (m + 1) * P)
                    for c in range(KM):
                        for n, (w, uT_part) in enumerate(((win_hi, uTh), (win_hi, uTl), (win_lo, uTh))):
                            last = nc.tensor.matmul(pA[i][:, 0:UW], w[:, c, cols], uT_part[s][:, c, :],
                                                    start=(c, n) == (0, 0), stop=(c, n) == (KM - 1, 2))
                    last.then_inc(conv_ps, 1)

            def dtT(k, _):
                need(pe, dtr_ready, passed(k, 1, 0))
                need(pe, conv_done, passed(k, CH, 0))
                for j in range(J):
                    last = transpose(pA[0][:, j * P:(j + 1) * P], dtr[:, j * P:(j + 1) * P])
                last.then_inc(dtT_ps, 1)

            def cum_sums(k, _):
                n = J * NH
                need(pe, dA_ready, passed(k, 1, 0))
                need(pe, conv_done, passed(k, CH, 1))
                for i, tri in enumerate((upper, ones, lower)):
                    last = nc.tensor.matmul(pA[1][:, i * n:(i + 1) * n], tri[:], dA[:].rearrange("p j h -> p (j h)"),
                                            start=True, stop=True)
                last.then_inc(cum_ps, 1)

            def cumT(k, _):
                need(pe, cum_ready, passed(k, 1, 0))
                need(pe, conv_done, passed(k, CH, 2))
                transpose(pA[0][0:J * NH, 0:P], cum[k[1]][:].rearrange("p j h -> p (j h)")).then_inc(cumT_ps, 1)

            def z(k, j):
                s = k[1]
                need(pe, conv_done, passed(k, CH, 3 if j == 0 else 4))
                for c in range(KM):
                    for n, (uT_part, w) in enumerate(((uTh, win_hi), (uTh, win_lo), (uTl, win_hi))):
                        last = nc.tensor.matmul(pA[1 - j][:], uT_part[s][:, c, CARRY + j * P:CARRY + (j + 1) * P],
                                                w[:, c, 0:DI], start=(c, n) == (0, 0), stop=(c, n) == (KM - 1, 2))
                last.then_inc(z_ps, 1)

            def front(k, j):
                s = k[1]
                cols = slice(j * P, (j + 1) * P)
                need(pe, xbc_ready, passed(k, 3, 2))
                if j == 0:
                    need(pe, u2Tl_ready, passed(back(k, 1), J, 1))
                else:
                    need(pe, gTl_ready, passed(k, J, 0))
                for m in range(XS):
                    last = transpose(pT[:, m * P:(m + 1) * P], xbc[s][:, m, cols])
                last.then_inc(xT_ps, 1)
                need(pe, bg_ready, passed(k if j else back(k, 1), J, 1 - j))
                transpose(pG[:, 0:P], xbc[s][:, XS, cols])
                nc.tensor.matmul(pG[:, P:2 * P], xbc[s][:, XS, cols], xbc[s][:, XS + 1, cols],
                                 start=True, stop=True).then_inc(g_ps, 1)

            def r_before(k, j):
                return passed(k if j else back(k, 1), J, 1 - j)

            def inter(k, j):
                if not first_tile(k, j):
                    need(pe, s_ready, state_count(k, j) + -1)
                    need(pe, r_ready, r_before(k, j))
                    nc.tensor.matmul(pY[:], xbc[k[1]][:, XS + 1, j * P:(j + 1) * P], S[:],
                                     start=True, stop=True).then_inc(inter_ps, 1)

            def intra(k, j):
                s = k[1]
                if first_tile(k, j):
                    need(pe, r_ready, r_before(k, j))
                else:
                    need(pe, t1_ready, inter_count(k, j))
                need(pe, mix_ready, passed(k, J, j))
                need(pe, xdt_ready, passed(k, J, j))
                for h in range(NH):
                    last = nc.tensor.matmul(pY[:, h * HD:(h + 1) * HD], R[s][:, j, h, :], xdt[j][:, h * HD:(h + 1) * HD],
                                            start=True, stop=True)
                last.then_inc(intra_ps, 1)

            def gateT(k, j):
                need(pe, g_ready, passed(k, J, j))
                if j == 0:
                    need(pe, xtok_ready, passed(k, J, 0))
                else:
                    need(pe, u2Tl_ready, passed(k, J, 0))
                for c in range(KI):
                    last = transpose(pT[:, c * P:(c + 1) * P], g[j][:, c * P:(c + 1) * P])
                last.then_inc(gT_ps, 1)

            def project(k, j):
                need(pe, y_ready, passed(k, J, j))
                need(pe, gTl_ready, passed(k, J, j))
                for c in range(KI):
                    for n, (gT_part, w) in enumerate(((gTh, wout_hi), (gTh, wout_lo), (gTl, wout_hi))):
                        last = nc.tensor.matmul(pY[:, 0:DM], gT_part[j][:, c, :], w[:, c, :],
                                                start=(c, n) == (0, 0), stop=(c, n) == (KI - 1, 2))
                last.then_inc(proj_ps, 1)

            def state(k, j):
                if not last_tile(k, j):
                    need(pe, xst_ready, state_count(k, j))
                    need(pe, s_ready, state_count(k, j) + -1)
                    nc.tensor.matmul(pS[:], bg[j][:, 0, :], xst[j][:], start=True, stop=True).then_inc(state_ps, 1)

            def u2T(k, j):
                need(pe, u2_ready, passed(k, J, j))
                if j == 0:
                    need(pe, xtok_ready, passed(k, J, 1))
                else:
                    need(pe, gTl_ready, passed(k, J, 1))
                for c in range(KM):
                    last = transpose(pT[:, c * P:(c + 1) * P], u2[j][:, c * P:(c + 1) * P])
                last.then_inc(u2T_ps, 1)

            def up(k, q):
                s = k[1]
                need(pe, u2Tl_ready, passed(k, J, J - 1))
                if q < 2:
                    need(pe, ffo_ready, passed(back(k, 1), J, q))
                else:
                    need(pe, gelu_ready, passed(k, KF, 2 * (q - 2) + 1))
                for i in range(2):
                    m = 2 * q + i
                    for c in range(KM):
                        for n, part in enumerate((u2Th, u2Tl)):
                            last = nc.tensor.matmul(pF[q % 2][:, i * HALF:(i + 1) * HALF],
                                                    w1_t[:, c * FF + m * P:c * FF + (m + 1) * P], part[s][:, c, :],
                                                    start=(c, n) == (0, 0), stop=(c, n) == (KM - 1, 1))
                last.then_inc(up_ps, 1)

            def down(k, j):
                need(pe, hl_ready, passed(k, 4, 3))
                need(pe, gelu_ready, passed(k, KF, 5 + 2 * j))
                for c in range(KF):
                    for n, part in enumerate((hh, hl)):
                        last = nc.tensor.matmul(pF[j][:, 0:DM], part[:, c, j * P:(j + 1) * P],
                                                w2_t[:, c * DM:(c + 1) * DM],
                                                start=(c, n) == (0, 0), stop=(c, n) == (KF - 1, 1))
                last.then_inc(down_ps, 1)

            run(pe, {("A", "uT"): uT, ("A", "dt"): dt, ("A", "conv"): conv_in, ("A", "dtT"): dtT, ("A", "cum"): cum_sums,
                     ("A", "cumT"): cumT, ("A", "z"): z, ("S", "front"): front, ("S", "inter"): inter,
                     ("S", "intra"): intra, ("S", "gateT"): gateT, ("S", "project"): project, ("S", "state"): state,
                     ("S", "norm2"): u2T, ("F", "up"): up, ("F", "down"): down})


def kernel(L0_attn_x, L0_attn_in_proj_w, L0_attn_conv_w, L0_attn_conv_b, L0_attn_dt_bias, L0_attn_A_log,
           L0_attn_D, L0_attn_norm_w, L0_attn_out_proj_w, L0_ffn_W1, L0_ffn_b1, L0_ffn_W2, L0_ffn_b2):
    import concourse.bacc as bacc
    from concourse.bass_utils import run_bass_kernel_spmd

    def by_partition(a):
        a = np.asarray(a)
        return np.moveaxis(a.reshape(a.shape[0] // P, P, *a.shape[1:]), 0, 1)

    arrays = {
        "x": L0_attn_x, "w_in": np.asarray(L0_attn_in_proj_w).T,
        "conv_w": by_partition(L0_attn_conv_w), "conv_b": by_partition(L0_attn_conv_b),
        "dt_bias": L0_attn_dt_bias, "a_log": L0_attn_A_log, "d_skip": L0_attn_D,
        "norm_w": by_partition(L0_attn_norm_w), "w_out": np.asarray(L0_attn_out_proj_w).T,
        "w1": np.asarray(L0_ffn_W1).T, "b1": by_partition(L0_ffn_b1),
        "w2": np.asarray(L0_ffn_W2).T, "b2": L0_ffn_b2,
    }
    arrays = {n: np.ascontiguousarray(a) for n, a in arrays.items()}
    nc = bacc.Bacc("TRN2", target_bir_lowering=False, num_devices=1)
    aps = [nc.dram_tensor(n, a.shape, mybir.dt.from_np(a.dtype), kind="ExternalInput").ap()
           for n, a in arrays.items()]
    heads = arrays["dt_bias"].shape[0]
    cum_dram = nc.dram_tensor("cum_dram", (2, 2 * heads, P), F32, kind="Internal").ap()
    out = nc.dram_tensor("out", arrays["x"].shape, F32, kind="ExternalOutput").ap()
    build(nc, *aps, cum_dram, out)
    r = run_bass_kernel_spmd(nc, [arrays], core_ids=[0])
    return r.results[0]["out"]
```

```python
from contextlib import ExitStack

import numpy as np
import concourse.bass as bass
from concourse import mybir

F32 = mybir.dt.float32
F32R = mybir.dt.float32r
ALU = mybir.AluOpType
ACT = mybir.ActivationFunctionType
AX = mybir.AxisListType

P = 128
CONSTS = 14
SP_STEPS = 15
CARRY = 4
EPS = 1e-5

STEP = [
    ("mix", 1, 3), ("sums token", 0, 2), ("inter decay", 1, 3), ("z silu", 1, 2), ("up", 0, 4),
    ("ln1 stats", 0, 1), ("ffn stats", 0, 5), ("sums back", 0, 2), ("gate rsqrt", 0, 3), ("add inter", 1, 3),
    ("ffn rsqrt", 0, 5), ("project", 0, 3), ("attn out", 0, 3), ("attn stats", 0, 3), ("attn rsqrt", 0, 3),
    ("ffn norm", 0, 5), ("gelu", 0, 4), ("decay", 0, 2), ("intra", 1, 3), ("y", 1, 3), ("hidden hi", 0, 4),
    ("attn norm", 0, 3), ("conv", 2, 2), ("conv first", 2, 2), ("scale state", 1, 3), ("up", 1, 4),
    ("up", 2, 4), ("ln1 rsqrt", 0, 1), ("gelu", 1, 4), ("u", 0, 1), ("hidden lo", 0, 4), ("gate", 1, 3),
    ("hidden hi", 1, 4), ("gelu", 2, 4), ("conv taps", 2, 2), ("state", 1, 3), ("new state", 1, 3),
    ("gateT", 1, 3), ("gate hi", 1, 3), ("hidden hi", 2, 4), ("up", 3, 4), ("uT", 0, 1), ("u hi", 0, 1),
    ("gate lo", 1, 3), ("store", 0, 6), ("add ffn", 0, 5), ("hidden lo", 1, 4), ("add residual", 0, 3),
    ("gate square", 1, 3), ("project", 1, 3), ("gelu", 3, 4), ("hidden lo", 2, 4), ("hidden hi", 3, 4),
    ("keep xu", 0, 2), ("ln2 stats", 0, 3), ("ln2 rsqrt", 0, 3), ("u lo", 0, 1), ("dt", 0, 1),
    ("dt rows", 0, 1), ("gate mean", 1, 3), ("gate rsqrt", 1, 3), ("ffn stats", 1, 5), ("ffn rsqrt", 1, 5),
    ("u2", 0, 3), ("hidden lo", 3, 4), ("u2T", 0, 3), ("conv", 0, 1), ("attn out", 1, 3), ("attn stats", 1, 3),
    ("conv silu", 1, 2), ("attn rsqrt", 1, 3), ("ffn norm", 1, 5), ("u2 hi", 0, 3), ("conv silu", 2, 2),
    ("conv first", 0, 1), ("store", 1, 6), ("u2 lo", 0, 3), ("xT and G", 0, 2), ("attn norm", 1, 3),
    ("add ffn", 1, 5), ("add residual", 1, 3), ("keep xu", 1, 2), ("load x", 0, 0), ("inter", 0, 2),
    ("dt decay", 0, 2), ("conv taps", 0, 1), ("ln2 stats", 1, 3), ("down", 0, 4), ("x token", 0, 2),
    ("conv silu", 0, 1), ("x for state", 0, 2), ("B and G", 0, 2), ("dtT", 0, 1), ("scale state", 0, 2),
    ("dt token", 0, 1), ("softplus in", 0, 1), ("z", 0, 1), ("ln2 rsqrt", 1, 3), ("z silu", 0, 1),
    ("softplus exp", 0, 1), ("u2", 1, 3), ("state", 0, 2), ("u2T", 1, 3), ("x dt", 0, 2), ("new state", 0, 2),
    ("conv", 1, 1), ("inter decay", 0, 2), ("down", 1, 4), ("softplus", 0, 1), ("softplus", 1, 1),
    ("softplus", 2, 1), ("softplus", 3, 1), ("decay exp", 0, 2), ("softplus", 4, 1), ("u2 hi", 1, 3),
    ("u2 lo", 1, 3), ("conv first", 1, 1), ("softplus", 5, 1), ("decay", 1, 2), ("xT and G", 1, 2),
    ("x token", 1, 2), ("B and G", 1, 2), ("skip", 0, 2), ("mask", 0, 2), ("mix", 0, 2), ("intra", 0, 2),
    ("add inter", 0, 2), ("conv taps", 1, 1), ("y", 0, 2), ("sums", 0, 1), ("sums head", 0, 1), ("gate", 0, 2),
    ("x dt", 1, 2), ("decay exp", 1, 2), ("z", 1, 1), ("ffn out", 0, 4), ("ffn out", 1, 4), ("gateT", 0, 2),
    ("gate square", 0, 2), ("x for state", 1, 2), ("skip", 1, 2), ("gate hi", 0, 2), ("gate lo", 0, 2),
    ("sumsT", 0, 1), ("sums out", 0, 1), ("mask", 1, 2), ("gate mean", 0, 2), ("inter", 1, 2),
]
LAG = max(lag for _, _, lag in STEP)


def build(nc, x, w_in, conv_w, conv_b, dt_bias, a_log, d_skip, norm_w, w_out, w1, b1, w2, b2,
          cum_dram, out):
    B, L, DM = x.shape
    KM = DM // P
    DIN = w_in.shape[1]
    DI = w_out.shape[0]
    KI = DI // P
    NH = dt_bias.shape[0]
    HD = DI // NH
    CH = conv_w.shape[1]
    TAPS = conv_w.shape[2]
    XS = KI
    FF = w1.shape[1]
    KF = FF // P
    HALF = L // 2
    J = HALF // P
    UW = CARRY + HALF
    assert (KM, KI, CH, J, KF, TAPS, L // HALF) == (2, 4, 6, 2, 8, 4, 2)

    xv = x.rearrange("b (s j p) d -> b s p j d", s=2, p=P)
    ov = out.rearrange("b (s j p) d -> b s j p d", s=2, p=P)

    with ExitStack() as ctx:
        def sb(name, shape, dt=F32):
            return ctx.enter_context(nc.sbuf_tensor(name, shape, dt))

        def bank(name):
            return ctx.enter_context(nc.psum_tensor(name, [P, 512], F32))

        def sem(name):
            return ctx.enter_context(nc.semaphore(name))

        win_f = sb("win_f", [P, KM, DIN])
        win_hi = sb("win_hi", [P, KM, DIN], F32R)
        win_lo = sb("win_lo", [P, KM, DIN], F32R)
        wdt = sb("wdt", [P, KM, P], F32R)
        wout_hi = sb("wout_hi", [P, KI, DM], F32R)
        wout_lo = sb("wout_lo", [P, KI, DM], F32R)
        w1_t = sb("w1_t", [P, KM * FF], F32R)
        w2_t = sb("w2_t", [P, KF * DM], F32R)
        convw = sb("convw", [P, CH, TAPS])
        convb = sb("convb", [P, CH])
        b1s = sb("b1s", [P, KF])
        nws = sb("nws", [P, KI])
        b2s = sb("b2s", [P, DM])
        dtb = sb("dtb", [P, NH])
        a_pos = sb("a_pos", [P, NH])
        dsk = sb("dsk", [P, NH])
        ident = sb("ident", [P, P])
        tri = sb("tri", [P, 2, P])
        upper, lower = tri[:, 0, :], tri[:, 1, :]
        ones = sb("ones", [P, P])
        mhalf = sb("mhalf", [P, J])
        absum = sb("absum", [P, 2])
        thr = sb("thr", [P, 2])
        nthr = sb("nthr", [P, 2])
        XU = [sb(f"XU{s}", [P, J, 2, DM]) for s in range(2)]
        XR = [sb(f"XR{j}", [P, 2, DM]) for j in range(J)]
        st1 = sb("st1", [P, J, 6])
        mv1 = sb("mv1", [P, J, 2])
        ve1 = sb("ve1", [P, J])
        rs1 = sb("rs1", [P, J])
        uTh = [sb(f"uTh{s}", [P, KM, UW], F32R) for s in range(2)]
        uTl = [sb(f"uTl{s}", [P, KM, UW], F32R) for s in range(2)]
        acc = [sb(f"acc{q}", [P, 2, HALF]) for q in range(2)]
        xbc = [sb(f"xbc{s}", [P, CH, HALF]) for s in range(2)]
        sz = [sb(f"sz{s}", [P, J, DI]) for s in range(2)]
        dtr = sb("dtr", [P, HALF])
        dtt = sb("dtt", [P, J, 2 * NH])
        sp = sb("sp", [P, 8, J, NH])
        dts = [sb(f"dts{s}", [P, J, NH]) for s in range(2)]
        dA = sb("dA", [P, P])
        cr = sb("cr", [P, 2, P])
        cum = [sb(f"cum{s}", [P, J, NH]) for s in range(2)]
        ecum = [sb(f"ecum{s}", [P, 2, J, NH]) for s in range(2)]
        etot = [sb(f"etot{s}", [P, J, NH]) for s in range(2)]
        dtdec = [sb(f"dtdec{s}", [P, J, NH]) for s in range(2)]
        R = [sb(f"R{s}", [P, J, NH, P]) for s in range(2)]
        xtok = [sb(f"xtok{j}", [P, DI]) for j in range(J)]
        bg = [sb(f"bg{j}", [P, 2, P]) for j in range(J)]
        gm = [sb(f"gm{j}", [P, P]) for j in range(J)]
        xdt = [sb(f"xdt{j}", [P, DI]) for j in range(J)]
        xst = [sb(f"xst{j}", [P, DI]) for j in range(J)]
        xd = [sb(f"xd{j}", [P, DI]) for j in range(J)]
        t1 = [sb(f"t1{j}", [P, DI]) for j in range(J)]
        g = [sb(f"g{j}", [P, DI]) for j in range(J)]
        S = sb("S", [P, DI])
        sqj = sb("sqj", [P, DI])
        ss = sb("ss", [P, J])
        vg = sb("vg", [P, J])
        rg = sb("rg", [P, J])
        gTh = [sb(f"gTh{j}", [P, KI, P], F32R) for j in range(J)]
        gTl = [sb(f"gTl{j}", [P, KI, P], F32R) for j in range(J)]
        r = [sb(f"r{j}", [P, DM]) for j in range(J)]
        sta = sb("sta", [P, J, 6])
        mva = sb("mva", [P, J, 2])
        vea = sb("vea", [P, J])
        rsa = sb("rsa", [P, J])
        x1 = [sb(f"x1{s}", [P, J, DM]) for s in range(2)]
        st2 = sb("st2", [P, J, 6])
        mv2 = sb("mv2", [P, J, 2])
        ve2 = sb("ve2", [P, J])
        rs2 = sb("rs2", [P, J])
        u2 = [sb(f"u2{j}", [P, DM]) for j in range(J)]
        u2Th = [sb(f"u2Th{s}", [P, KM, HALF], F32R) for s in range(2)]
        u2Tl = [sb(f"u2Tl{s}", [P, KM, HALF], F32R) for s in range(2)]
        hf = [sb(f"hf{q}", [P, 2, HALF]) for q in range(2)]
        hh = sb("hh", [P, KF, HALF], F32R)
        hl = sb("hl", [P, KF, HALF], F32R)
        ffo = [sb(f"ffo{j}", [P, DM]) for j in range(J)]
        stf = sb("stf", [P, J, 6])
        mvf = sb("mvf", [P, J, 2])
        vef = sb("vef", [P, J])
        rsf = sb("rsf", [P, J])
        ob = [sb(f"ob{j}", [P, DM]) for j in range(J)]

        wout_f = xbc[0][:].rearrange("p c t -> p (c t)")[:, 0:KI * DM].rearrange("p (c n) -> p c n", c=KI)
        w1_f = R[0][:].rearrange("p j h i -> p (j h i)")
        w2_f = R[1][:].rearrange("p j h i -> p (j h i)")

        pA = [bank(f"pA{i}") for i in range(2)]
        pT = bank("pT")
        pG = bank("pG")
        pY = bank("pY")
        pS = bank("pS")
        pF = [bank(f"pF{i}") for i in range(2)]

        w_ld = {n: sem(f"{n}_ld") for n in ("win", "wout", "w1", "w2", "small")}
        x_ld = [sem(f"x_ld{s}") for s in range(2)]
        xr_ld = [sem(f"xr_ld{j}") for j in range(J)]
        cum_st = sem("cum_st")
        r_ld = [sem(f"r_ld{s}") for s in range(2)]
        out_st = [sem(f"out_st{j}") for j in range(J)]
        consts = sem("consts")
        prep = sem("prep")
        absum_ready = sem("absum_ready")
        absum_ps = sem("absum_ps")
        weights_ready = sem("weights_ready")
        a_exp = sem("a_exp")
        ln1_mv = sem("ln1_mv")
        ln1_ve = sem("ln1_ve")
        ln1_rstd = sem("ln1_rstd")
        u_ready = sem("u_ready")
        uT_ps = sem("uT_ps")
        uTh_ready = sem("uTh_ready")
        uTl_ready = sem("uTl_ready")
        dt_ps = sem("dt_ps")
        dtr_ready = sem("dtr_ready")
        conv_ps = sem("conv_ps")
        conv_first = sem("conv_first")
        conv_tap = sem("conv_tap")
        conv_done = sem("conv_done")
        xbc_ready = sem("xbc_ready")
        dtT_ps = sem("dtT_ps")
        dtt_ready = sem("dtt_ready")
        sp_step = sem("sp_step")
        sp_exp = sem("sp_exp")
        dA_ready = sem("dA_ready")
        cum_ps = sem("cum_ps")
        cum_ready = sem("cum_ready")
        ecum_ready = sem("ecum_ready")
        etot_ready = sem("etot_ready")
        dtdec_ready = sem("dtdec_ready")
        cumT_ps = sem("cumT_ps")
        cr_ready = sem("cr_ready")
        z_ps = sem("z_ps")
        sz_ready = sem("sz_ready")
        xT_ps = sem("xT_ps")
        g_ps = sem("g_ps")
        xtok_ready = sem("xtok_ready")
        bg_ready = sem("bg_ready")
        gm_ready = sem("gm_ready")
        xdt_ready = sem("xdt_ready")
        xst_ready = sem("xst_ready")
        xd_ready = sem("xd_ready")
        diff_ready = sem("diff_ready")
        exp_ready = sem("exp_ready")
        mix_ready = sem("mix_ready")
        inter_ps = sem("inter_ps")
        t1_ready = sem("t1_ready")
        yx_ready = sem("yx_ready")
        intra_ps = sem("intra_ps")
        y_ready = sem("y_ready")
        g_ready = sem("g_ready")
        ss_ready = sem("ss_ready")
        vg_ready = sem("vg_ready")
        rg_ready = sem("rg_ready")
        gT_ps = sem("gT_ps")
        gTh_ready = sem("gTh_ready")
        gTl_ready = sem("gTl_ready")
        proj_ps = sem("proj_ps")
        r_ready = sem("r_ready")
        state_ps = sem("state_ps")
        s_scaled = sem("s_scaled")
        s_ready = sem("s_ready")
        lna_mv = sem("lna_mv")
        lna_ve = sem("lna_ve")
        lna_rstd = sem("lna_rstd")
        rn_ready = sem("rn_ready")
        x1_ready = sem("x1_ready")
        ln2_mv = sem("ln2_mv")
        ln2_ve = sem("ln2_ve")
        ln2_rstd = sem("ln2_rstd")
        u2_ready = sem("u2_ready")
        u2T_ps = sem("u2T_ps")
        u2Th_ready = sem("u2Th_ready")
        u2Tl_ready = sem("u2Tl_ready")
        up_ps = sem("up_ps")
        gelu_ready = sem("gelu_ready")
        hh_ready = sem("hh_ready")
        hl_ready = sem("hl_ready")
        down_ps = sem("down_ps")
        ffo_ready = sem("ffo_ready")
        lnf_mv = sem("lnf_mv")
        lnf_ve = sem("lnf_ve")
        lnf_rstd = sem("lnf_rstd")
        fn_ready = sem("fn_ready")
        ob_ready = sem("ob_ready")

        def passed(k, n, i):
            return k[0] * (2 * n) + (k[1] * n + i + 1)

        def need(eng, s, count):
            if not isinstance(count, int) or count > 0:
                eng.wait_ge(s, count)

        def back(k, n):
            h = k[1] - n
            return (k[0] + h // 2, h % 2)

        def first_tile(k, j):
            return (k[1], j) == (0, 0)

        def last_tile(k, j):
            return (k[1], j) == (1, J - 1)

        def inter_count(k, j):
            return 3 * k[0] + 2 * k[1] + j

        def state_count(k, j):
            return 3 * k[0] + 2 * k[1] + j + 1

        def half(t):
            return (t // 2, t % 2)

        def final(k):
            return isinstance(k[0], int) and k == (B - 1, 1)

        def run(eng, parts):
            def step(k, check=None):
                for part, arg, lag in STEP:
                    if part in parts and (check is None or 0 <= check - lag < 2 * B):
                        parts[part](back(k, lag), arg)

            first = LAG // 2 + 2
            for t in range(2 * first):
                step(half(t), t)
            with eng.Fori(first, B) as b:
                step((b, 0))
                step((b, 1))
            for t in range(2 * B, 2 * B + LAG):
                step(half(t), t)

        block = ctx.enter_context(nc.Block())

        @block.sync
        def _(sy):
            sy.dma_start(win_f[:], w_in.rearrange("(c p) n -> p c n", p=P)).then_inc(w_ld["win"], 16)
            sy.dma_start(convw[:], conv_w).then_inc(w_ld["small"], 16)
            sy.dma_start(convb[:], conv_b).then_inc(w_ld["small"], 16)
            sy.dma_start(b1s[:], b1).then_inc(w_ld["small"], 16)
            sy.dma_start(nws[:], norm_w).then_inc(w_ld["small"], 16)
            for dst, src in ((b2s, b2), (dtb, dt_bias), (a_pos, a_log), (dsk, d_skip)):
                sy.dma_start(dst[:], src.partition_broadcast(P)).then_inc(w_ld["small"], 16)
            sy.dma_start(wout_f, w_out.rearrange("(c p) n -> p c n", p=P)).then_inc(w_ld["wout"], 16)
            sy.dma_start(w1_f.rearrange("p (c n) -> p c n", c=KM),
                         w1.rearrange("(c p) n -> p c n", p=P)).then_inc(w_ld["w1"], 16)
            sy.dma_start(w2_f.rearrange("p (c n) -> p c n", c=KF),
                         w2.rearrange("(c p) n -> p c n", p=P)).then_inc(w_ld["w2"], 16)

            def load_x(k, _):
                for j in range(J):
                    need(sy, xr_ld[j], passed(back(k, 2), 16, 15))
                sy.dma_start(XU[k[1]][:, :, 0, :], xv[k[0], k[1]]).then_inc(x_ld[k[1]], 16)

            def keep_xu(k, j):
                need(sy, x1_ready, passed(back(k, 1), J, j))
                sy.dma_start(XR[j][:], XU[k[1]][:, j]).then_inc(xr_ld[j], 16)

            def sums_out(k, _):
                need(sy, cr_ready, passed(k, 1, 0))
                sy.dma_start(cum_dram[k[1]], cr[0:J * NH, 0, :]).then_inc(cum_st, 16)

            def sums_back(k, _):
                sy.wait_ge(cum_st, passed(k, 16, 15))
                need(sy, intra_ps, passed(back(k, 2), J, J - 1))
                sy.dma_start(R[k[1]][:].rearrange("p j h i -> p (j h i)"),
                             cum_dram[k[1]].rearrange("a i -> (a i)").partition_broadcast(P)
                             ).then_inc(r_ld[k[1]], 16)

            def store(k, j):
                need(sy, ob_ready, passed(k, J, j))
                sy.dma_start(ov[k[0], k[1], j], ob[j][:]).then_inc(out_st[j], 16)

            run(sy, {"load x": load_x, "keep xu": keep_xu, "sums out": sums_out, "sums back": sums_back,
                     "store": store})
            for j in range(J):
                sy.wait_ge(out_st[j], 16 * 2 * B)

        @block.gpsimd
        def _(pool):
            nc.gpsimd.memset(ident[:], 0.0).then_inc(consts, 1)
            nc.gpsimd.memset(upper, 1.0).then_inc(consts, 1)
            nc.gpsimd.memset(lower, 1.0).then_inc(consts, 1)
            nc.gpsimd.memset(ones[:], 1.0).then_inc(consts, 1)
            nc.gpsimd.memset(mhalf[:], -0.5).then_inc(consts, 1)
            for s in range(2):
                nc.gpsimd.memset(uTh[s][:, :, 0:CARRY].bitcast(F32), 0.0).then_inc(consts, 1)
                nc.gpsimd.memset(uTl[s][:, :, 0:CARRY].bitcast(F32), 0.0).then_inc(consts, 1)
            nc.gpsimd.memset(wdt[:].bitcast(F32), 0.0).then_inc(consts, 1)
            nc.gpsimd.memset(dA[:], 0.0).then_inc(consts, 1)
            pool.wait_ge(consts, 5)
            nc.gpsimd.affine_select(out=ident[:], in_=ident[:], compare_op=ALU.not_equal, fill=1.0,
                                    base=0, pattern=[[-1, P]], channel_multiplier=1).then_inc(consts, 1)
            nc.gpsimd.affine_select(out=upper, in_=upper, compare_op=ALU.is_ge, fill=0.0,
                                    base=0, pattern=[[1, P]], channel_multiplier=-1).then_inc(consts, 1)

            nc.gpsimd.affine_select(out=lower, in_=lower, compare_op=ALU.is_ge, fill=0.0,
                                    base=-1, pattern=[[-1, P]], channel_multiplier=1).then_inc(consts, 1)
            pool.wait_ge(consts, CONSTS)

            def rstd(ve_ready, rstd_ready, ve, rs, k, n, i, cols):
                need(pool, ve_ready, passed(k, n, i))
                nc.gpsimd.tensor_tensor(rs[:, cols], ve[:, cols], mhalf[:, 0:cols.stop - cols.start],
                                        ALU.pow).then_inc(rstd_ready, 1)

            def ln1_rsqrt(k, _):
                need(pool, u_ready, passed(back(k, 1), J, J - 1))
                rstd(ln1_ve, ln1_rstd, ve1, rs1, k, 1, 0, slice(0, J))

            def mask(k, j):
                need(pool, bg_ready, passed(k, J, j))
                need(pool, mix_ready, passed(back(k, 1), J, j))
                nc.gpsimd.tensor_tensor(gm[j][:], bg[j][:, 1, :], upper, ALU.mult).then_inc(gm_ready, 1)

            def by_head(ap):
                return ap.rearrange("p (h d) -> p h d", h=NH)

            def x_for_state(k, j):
                b, s = k
                if not last_tile(k, j):
                    need(pool, xtok_ready, passed(k, J, j))
                    need(pool, dtdec_ready, passed(k, 1, 0))
                    need(pool, state_ps, 3 * b + (-1 if (s, j) == (0, 1) else s))
                    nc.gpsimd.tensor_tensor(by_head(xst[j][:]), by_head(xtok[j][:]),
                                            dtdec[s][:, j, :].unsqueeze(2).to_broadcast([P, NH, HD]),
                                            ALU.mult).then_inc(xst_ready, 1)

            def skip_term(k, j):
                need(pool, xtok_ready, passed(k, J, j))
                need(pool, y_ready, passed(back(k, 1), J, j))
                nc.gpsimd.tensor_tensor(by_head(xd[j][:]), by_head(xtok[j][:]),
                                        dsk[:].unsqueeze(2).to_broadcast([P, NH, HD]),
                                        ALU.mult).then_inc(xd_ready, 1)

            def mix(k, j):
                need(pool, exp_ready, passed(k, J, j))
                pool.wait_ge(gm_ready, passed(k, J, j))
                nc.gpsimd.tensor_tensor(R[k[1]][:, j], R[k[1]][:, j],
                                        gm[j][:].unsqueeze(1).to_broadcast([P, NH, P]),
                                        ALU.mult).then_inc(mix_ready, 1)

            def add_inter(k, j):
                if not first_tile(k, j):
                    need(pool, t1_ready, inter_count(k, j))
                    pool.wait_ge(xd_ready, passed(k, J, j))
                    nc.gpsimd.tensor_tensor(xd[j][:], t1[j][:], xd[j][:], ALU.add).then_inc(yx_ready, 1)

            def gate_rsqrt(k, j):
                rstd(vg_ready, rg_ready, vg, rg, k, J, j, slice(j, j + 1))

            def attn_rsqrt(k, j):
                rstd(lna_ve, lna_rstd, vea, rsa, k, J, j, slice(j, j + 1))

            def add_residual(k, j):
                need(pool, rn_ready, passed(k, J, j))
                need(pool, xr_ld[j], passed(k, 16, 15))
                need(pool, ob_ready, passed(back(k, 2), J, j))
                nc.gpsimd.tensor_tensor(x1[k[1]][:, j], XR[j][:, 0, :], r[j][:], ALU.add).then_inc(x1_ready, 1)

            def ln2_rsqrt(k, j):
                rstd(ln2_ve, ln2_rstd, ve2, rs2, k, J, j, slice(j, j + 1))

            def hidden_lo(k, q):
                need(pool, hh_ready, passed(k, 4, q))
                nc.gpsimd.tensor_tensor(hl[:, 2 * q:2 * q + 2, :], hf[q % 2][:],
                                        hh[:, 2 * q:2 * q + 2, :].bitcast(F32),
                                        ALU.subtract).then_inc(hl_ready, 1)

            def ffn_rsqrt(k, j):
                rstd(lnf_ve, lnf_rstd, vef, rsf, k, J, j, slice(j, j + 1))

            def add_ffn(k, j):
                need(pool, fn_ready, passed(k, J, j))
                need(pool, out_st[j], passed(back(k, 1), 16, 15))
                nc.gpsimd.tensor_tensor(ob[j][:], x1[k[1]][:, j], ffo[j][:], ALU.add).then_inc(ob_ready, 1)

            run(pool, {"ln1 rsqrt": ln1_rsqrt, "mask": mask, "x for state": x_for_state, "skip": skip_term,
                       "mix": mix, "add inter": add_inter, "gate rsqrt": gate_rsqrt, "attn rsqrt": attn_rsqrt,
                       "add residual": add_residual, "ln2 rsqrt": ln2_rsqrt, "hidden lo": hidden_lo,
                       "ffn rsqrt": ffn_rsqrt, "add ffn": add_ffn})

        @block.vector
        def _(dve):
            dve.wait_ge(w_ld["win"], 16)
            nc.vector.tensor_copy(win_hi[:], win_f[:]).then_inc(prep, 1)
            dve.wait_ge(prep, 1)
            nc.vector.tensor_tensor(win_lo[:], win_f[:], win_hi[:].bitcast(F32), ALU.subtract).then_inc(prep, 1)
            dve.wait_ge(prep, 2)
            dve.wait_ge(consts, CONSTS)
            nc.vector.tensor_copy(wdt[:, :, 0:NH], win_hi[:, :, DIN - NH:DIN].bitcast(F32)).then_inc(prep, 1)
            nc.vector.tensor_copy(wdt[:, :, NH:2 * NH], win_lo[:, :, DIN - NH:DIN].bitcast(F32)).then_inc(prep, 1)
            dve.wait_ge(w_ld["wout"], 16)
            for c in range(KI):
                nc.vector.tensor_scalar(wout_f[:, c, :], wout_f[:, c, :], nws[:, c:c + 1], None,
                                        ALU.mult).then_inc(prep, 1)
            dve.wait_ge(prep, 4 + KI)
            nc.vector.tensor_copy(wout_hi[:], wout_f).then_inc(prep, 1)
            dve.wait_ge(prep, 5 + KI)
            nc.vector.tensor_tensor(wout_lo[:], wout_f, wout_hi[:].bitcast(F32), ALU.subtract).then_inc(prep, 1)
            for n, (name, wf) in enumerate((("w1", w1_f), ("w2", w2_f))):
                dve.wait_ge(w_ld[name], 16)
                nc.vector.tensor_reduce(absum[:, n:n + 1], wf, axis=AX.X, op=ALU.add,
                                        apply_absolute_value=True).then_inc(absum_ready, 1)
            dve.wait_ge(absum_ps, 1)
            nc.vector.tensor_scalar(thr[:], pG[:, 0:2], 1.0 / (DM * FF), 1e-8, ALU.mult, ALU.max).then_inc(prep, 1)
            dve.wait_ge(prep, 7 + KI)
            nc.vector.tensor_scalar(nthr[:], thr[:], -0.5, None, ALU.mult).then_inc(prep, 1)
            nc.vector.tensor_scalar(thr[:], thr[:], 0.5, None, ALU.mult).then_inc(prep, 1)
            dve.wait_ge(prep, 9 + KI)
            for n, (wf, wt) in enumerate(((w1_f, w1_t), (w2_f, w2_t))):
                nc.vector.tensor_scalar(wt[:], wf, nthr[:, n:n + 1], 1.0, ALU.is_ge,
                                        ALU.subtract).then_inc(prep, 1)
                dve.wait_ge(prep, 10 + KI + 2 * n)
                nc.vector.scalar_tensor_tensor(wt[:], wf, thr[:, n:n + 1], wt[:].bitcast(F32), ALU.is_gt,
                                               ALU.add).then_inc(prep, 1)
            dve.wait_ge(prep, 13 + KI)
            dve.wait_ge(a_exp, 1)
            nc.vector.memset(sp[:], 0.0).then_inc(weights_ready, 1)
            dve.wait_ge(weights_ready, 1)

            def norm_tail(st, mv, ve, s_mv, s_ve, k, j):
                dve.drain()
                nc.vector.bn_aggr(mv[:, j, :], st[:, j, :]).then_inc(s_mv, 1)
                dve.wait_ge(s_mv, passed(k, J, j))
                nc.vector.tensor_scalar(ve[:, j:j + 1], mv[:, j, 1:2], EPS, None, ALU.add).then_inc(s_ve, 1)

            def normalize(dst, src, mv, rs, j, done):
                nc.vector.tensor_scalar(dst, src, mv[:, j, 0:1], rs[:, j:j + 1], ALU.subtract,
                                        ALU.mult).then_inc(done, 1)

            def by_head(ap):
                return ap.rearrange("p (h d) -> p h d", h=NH)

            def per_head(ap):
                return ap.unsqueeze(2).to_broadcast([P, NH, HD])

            def ln1_stats(k, _):
                dve.wait_ge(x_ld[k[1]], 16 * (k[0] + 1))
                for j in range(J):
                    nc.vector.bn_stats(st1[:, j, :], XU[k[1]][:, j, 0, :])
                for j in range(J):
                    if j == 0:
                        dve.drain()
                    nc.vector.bn_aggr(mv1[:, j, :], st1[:, j, :]).then_inc(ln1_mv, 1)
                dve.wait_ge(ln1_mv, passed(k, J, J - 1))
                nc.vector.tensor_scalar(ve1[:], mv1[:, :, 1], EPS, None, ALU.add).then_inc(ln1_ve, 1)

            def u(k, _):
                need(dve, ln1_rstd, passed(k, 1, 0))
                for j in range(J):
                    normalize(XU[k[1]][:, j, 1, :], XU[k[1]][:, j, 0, :], mv1, rs1, j, u_ready)

            def u_lo(k, _):
                s = k[1]
                need(dve, uTh_ready, passed(k, 1, 0))
                if s == 1:
                    need(dve, uTl_ready, passed(back(k, 1), 1, 0))
                    nc.vector.tensor_copy(uTl[1][:, :, 0:CARRY], uTl[0][:, :, UW - CARRY:UW].bitcast(F32))
                nc.vector.tensor_tensor(uTl[s][:, :, CARRY:UW],
                                        pA[0][:].rearrange("p (c t) -> p c t", c=KM),
                                        uTh[s][:, :, CARRY:UW].bitcast(F32),
                                        ALU.subtract).then_inc(uTl_ready, 1)

            def conv(k, q):
                for tap in range(1, TAPS):
                    for c in range(2):
                        m = 2 * q + c
                        if tap == 1:
                            need(dve, conv_first, passed(k, CH, m))
                        else:
                            dve.wait_ge(conv_tap, passed(k, 2 * CH, 4 * q + 2 * (tap - 2) + c))
                        w = TAPS - 1 - tap
                        nc.vector.scalar_tensor_tensor(
                            acc[q % 2][:, c, :], pA[c][:, 1 + w:1 + w + HALF], convw[:, m, w:w + 1],
                            acc[q % 2][:, c, :], ALU.mult, ALU.add
                        ).then_inc(conv_done if tap == TAPS - 1 else conv_tap, 1)

            def sp_did(k, i):
                dve.wait_ge(sp_step, passed(k, SP_STEPS, i))

            def softplus_front(k, _):
                v, a = sp[:, 0], sp[:, 1]
                need(dve, dtt_ready, passed(k, 1, 0))
                nc.vector.tensor_tensor(v, dtt[:, :, 0:NH], dtt[:, :, NH:2 * NH], ALU.add).then_inc(sp_step, 1)
                sp_did(k, 0)
                nc.vector.tensor_tensor(v, v, dtb[:].unsqueeze(1).to_broadcast([P, J, NH]), ALU.add).then_inc(sp_step, 1)
                sp_did(k, 1)
                nc.vector.scalar_tensor_tensor(a, v, -1.0, v, ALU.mult, ALU.max).then_inc(sp_step, 1)

            def softplus_back(k, n):
                v, e, d, rc, z, qq, p = (sp[:, i] for i in (0, 2, 3, 4, 5, 6, 7))

                def series(i, odd):
                    sp_did(k, i - 1)
                    nc.vector.scalar_tensor_tensor(p, p, 1.0 / odd, qq, ALU.add, ALU.mult).then_inc(sp_step, 1)

                if n == 0:
                    need(dve, sp_exp, passed(k, 1, 0))
                    nc.vector.tensor_scalar(d, e, 2.0, None, ALU.add).then_inc(sp_step, 1)
                    sp_did(k, 3)
                    nc.vector.reciprocal(rc, d).then_inc(sp_step, 1)
                elif n == 1:
                    sp_did(k, 4)
                    nc.vector.tensor_tensor(z, e, rc, ALU.mult).then_inc(sp_step, 1)
                    sp_did(k, 5)
                    nc.vector.tensor_tensor(qq, z, z, ALU.mult).then_inc(sp_step, 1)
                elif n == 2:
                    sp_did(k, 6)
                    nc.vector.tensor_scalar(p, qq, 1.0 / 11, None, ALU.mult).then_inc(sp_step, 1)
                    series(8, 9)
                elif n == 3:
                    series(9, 7)
                    series(10, 5)
                elif n == 4:
                    series(11, 3)
                    sp_did(k, 11)
                    nc.vector.scalar_tensor_tensor(p, p, 1.0, z, ALU.add, ALU.mult).then_inc(sp_step, 1)
                    nc.vector.tensor_scalar(d, v, 0.0, None, ALU.max).then_inc(sp_step, 1)
                else:
                    sp_did(k, 13)
                    nc.vector.scalar_tensor_tensor(dts[k[1]][:], p, 2.0, d, ALU.mult, ALU.add).then_inc(sp_step, 1)
                    sp_did(k, 14)
                    nc.vector.tensor_tensor(dA[:, 0:J * NH].rearrange("p (j h) -> p j h", j=J), dts[k[1]][:],
                                            a_pos[:].unsqueeze(1).to_broadcast([P, J, NH]),
                                            ALU.mult).then_inc(dA_ready, 1)

            def dt_decay(k, _):
                s = k[1]
                need(dve, ecum_ready, passed(k, 1, 0))
                nc.vector.tensor_tensor(etot[s][:], ecum[s][:, 0], ecum[s][:, 1], ALU.mult).then_inc(etot_ready, 1)
                nc.vector.tensor_tensor(dtdec[s][:], dts[s][:], ecum[s][:, 1], ALU.mult).then_inc(dtdec_ready, 1)

            def x_dt(k, j):
                need(dve, xtok_ready, passed(k, J, j))
                need(dve, intra_ps, passed(back(k, 1), J, j))
                nc.vector.tensor_tensor(by_head(xdt[j][:]), by_head(xtok[j][:]), per_head(dts[k[1]][:, j, :]),
                                        ALU.mult).then_inc(xdt_ready, 1)

            def inter(k, j):
                if not first_tile(k, j):
                    need(dve, inter_ps, inter_count(k, j))
                    nc.vector.tensor_tensor(by_head(t1[j][:]), by_head(pY[:]), per_head(ecum[k[1]][:, 0, j, :]),
                                            ALU.mult).then_inc(t1_ready, 1)

            def y(k, j):
                need(dve, intra_ps, passed(k, J, j))
                if first_tile(k, j):
                    need(dve, xd_ready, passed(k, J, j))
                else:
                    need(dve, yx_ready, inter_count(k, j))
                nc.vector.tensor_tensor(t1[j][:], pY[:], xd[j][:], ALU.add).then_inc(y_ready, 1)

            def gate(k, j):
                dve.wait_ge(y_ready, passed(k, J, j))
                need(dve, sz_ready, passed(k, J, j))
                nc.vector.tensor_tensor(g[j][:], t1[j][:], sz[k[1]][:, j, :], ALU.mult).then_inc(g_ready, 1)

            def gate_mean(k, j):
                need(dve, ss_ready, passed(k, J, j))
                nc.vector.tensor_scalar(vg[:, j:j + 1], ss[:, j:j + 1], 1.0 / DI, EPS, ALU.mult, ALU.add).then_inc(vg_ready, 1)

            def gate_lo(k, j):
                need(dve, gTh_ready, passed(k, J, j))
                nc.vector.tensor_tensor(gTl[j][:], pT[:].rearrange("p (c t) -> p c t", c=KI), gTh[j][:].bitcast(F32),
                                        ALU.subtract).then_inc(gTl_ready, 1)

            def attn_out(k, j):
                need(dve, proj_ps, passed(k, J, j))
                need(dve, rg_ready, passed(k, J, j))
                dve.wait_ge(xr_ld[j], passed(k, 16, 15))
                nc.vector.scalar_tensor_tensor(r[j][:], pS[:, 0:DM], rg[:, j:j + 1], XR[j][:, 1, :], ALU.mult,
                                               ALU.add).then_inc(r_ready, 1)

            def attn_stats(k, j):
                dve.wait_ge(r_ready, passed(k, J, j))
                nc.vector.bn_stats(sta[:, j, :], r[j][:])
                norm_tail(sta, mva, vea, lna_mv, lna_ve, k, j)

            def attn_norm(k, j):
                need(dve, lna_rstd, passed(k, J, j))
                normalize(r[j][:], r[j][:], mva, rsa, j, rn_ready)

            def scale_state(k, j):
                if not last_tile(k, j) and not first_tile(k, j):
                    need(dve, inter_ps, inter_count(k, j))
                    need(dve, s_ready, state_count(k, j) + -1)
                    need(dve, etot_ready, passed(k, 1, 0))
                    nc.vector.tensor_tensor(by_head(S[:]), by_head(S[:]), per_head(etot[k[1]][:, j, :]),
                                            ALU.mult).then_inc(s_scaled, 1)

            def new_state(k, j):
                b, s = k
                if last_tile(k, j):
                    return
                need(dve, state_ps, state_count(k, j))
                if first_tile(k, j):
                    need(dve, inter_ps, 3 * b)
                    nc.vector.tensor_copy(S[:], pS[:]).then_inc(s_ready, 1)
                else:
                    dve.wait_ge(s_scaled, 2 * b + 2 * s + j)
                    nc.vector.tensor_tensor(S[:], pS[:], S[:], ALU.add).then_inc(s_ready, 1)

            def ln2_stats(k, j):
                need(dve, x1_ready, passed(k, J, j))
                nc.vector.bn_stats(st2[:, j, :], x1[k[1]][:, j, :])
                norm_tail(st2, mv2, ve2, ln2_mv, ln2_ve, k, j)

            def u2_norm(k, j):
                need(dve, ln2_rstd, passed(k, J, j))
                normalize(u2[j][:], x1[k[1]][:, j, :], mv2, rs2, j, u2_ready)

            def u2_lo(k, j):
                need(dve, u2Th_ready, passed(k, J, j))
                cols = slice(j * P, (j + 1) * P)
                nc.vector.tensor_tensor(u2Tl[k[1]][:, :, cols], pG[:, 0:DM].rearrange("p (c t) -> p c t", c=KM),
                                        u2Th[k[1]][:, :, cols].bitcast(F32), ALU.subtract).then_inc(u2Tl_ready, 1)

            def ffn_out(k, j):
                need(dve, down_ps, passed(k, J, j))
                need(dve, ob_ready, passed(back(k, 1), J, j))
                nc.vector.tensor_tensor(ffo[j][:], pF[j][:, 0:DM], b2s[:], ALU.add).then_inc(ffo_ready, 1)

            def ffn_stats(k, j):
                dve.wait_ge(ffo_ready, passed(k, J, j))
                nc.vector.bn_stats(stf[:, j, :], ffo[j][:])
                norm_tail(stf, mvf, vef, lnf_mv, lnf_ve, k, j)

            def ffn_norm(k, j):
                need(dve, lnf_rstd, passed(k, J, j))
                normalize(ffo[j][:], ffo[j][:], mvf, rsf, j, fn_ready)

            run(dve, {"ln1 stats": ln1_stats, "u": u, "u lo": u_lo, "conv taps": conv,
                      "softplus in": softplus_front, "softplus": softplus_back, "dt decay": dt_decay,
                      "x dt": x_dt, "inter decay": inter, "y": y, "gate": gate, "gate mean": gate_mean,
                      "gate lo": gate_lo, "attn out": attn_out, "attn stats": attn_stats,
                      "attn norm": attn_norm, "scale state": scale_state, "new state": new_state,
                      "ln2 stats": ln2_stats, "u2": u2_norm, "u2 lo": u2_lo, "ffn out": ffn_out,
                      "ffn stats": ffn_stats, "ffn norm": ffn_norm})

        @block.scalar
        def _(act):
            act.wait_ge(w_ld["small"], 16 * 8)
            nc.scalar.activation(a_pos[:], a_pos[:], ACT.Exp).then_inc(a_exp, 1)
            act.wait_ge(consts, CONSTS)

            def uT_hi(k, _):
                s = k[1]
                need(act, uT_ps, passed(k, 1, 0))
                need(act, conv_ps, passed(back(k, 2), CH, CH - 1))
                if s == 1:
                    need(act, uTh_ready, passed(back(k, 1), 1, 0))
                    nc.scalar.copy(uTh[1][:, :, 0:CARRY], uTh[0][:, :, UW - CARRY:UW].bitcast(F32))
                nc.scalar.copy(uTh[s][:, :, CARRY:UW],
                               pA[0][:].rearrange("p (c t) -> p c t", c=KM)).then_inc(uTh_ready, 1)

            def dt_out(k, _):
                need(act, dt_ps, passed(k, 1, 0))
                need(act, dtT_ps, passed(back(k, 1), 1, 0))
                nc.scalar.copy(dtr[:], pA[1][:, 0:HALF]).then_inc(dtr_ready, 1)

            def conv_first_tap(k, q):
                need(act, xbc_ready, passed(k, 3, 0) if q == 2 else passed(back(k, 1), 3, 2 if q == 0 else 1))
                for c in range(2):
                    m = 2 * q + c
                    need(act, conv_ps, passed(k, CH, m))
                    nc.scalar.activation(acc[q % 2][:, c, :], pA[c][:, CARRY:UW], ACT.Identity,
                                         bias=convb[:, m:m + 1], scale=convw[:, m, TAPS - 1:TAPS]).then_inc(conv_first, 1)

            def silu(k, q):
                need(act, conv_done, passed(k, CH, 2 * q + 1))
                need(act, intra_ps, passed(back(k, 2), J, J - 1))
                nc.scalar.activation(xbc[k[1]][:, 2 * q:2 * q + 2, :], acc[q % 2][:], ACT.Silu).then_inc(xbc_ready, 1)

            def dt_token(k, _):
                need(act, dtT_ps, passed(k, 1, 0))
                need(act, sp_step, passed(back(k, 1), SP_STEPS, 0))
                nc.scalar.copy(dtt[:], pA[0][:, 0:J * P].rearrange("p (j n) -> p j n", j=J)[:, :, 0:2 * NH]).then_inc(dtt_ready, 1)

            def softplus_exp(k, _):
                need(act, sp_step, passed(k, SP_STEPS, 2))
                nc.scalar.activation(sp[:, 2], sp[:, 1], ACT.Exp, scale=-1.0).then_inc(sp_exp, 1)

            def sums_head(k, _):
                need(act, cum_ps, passed(k, 1, 0))
                need(act, cum_st, passed(back(k, 1), 16, 15))
                need(act, cumT_ps, passed(back(k, 1), 1, 0))
                nc.scalar.copy(cr[:].rearrange("p a i -> p (a i)"), pA[0][:, 0:2 * P]).then_inc(cr_ready, 1)

            def sums_token(k, _):
                n = J * NH
                need(act, cumT_ps, passed(k, 1, 0))
                nc.scalar.mul(cum[k[1]][:].rearrange("p j h -> p (j h)"), pA[0][:, 0:n], -1.0).then_inc(cum_ready, 1)
                nc.scalar.activation(ecum[k[1]][:].rearrange("p a j h -> p a (j h)"),
                                     pA[0][:, 0:2 * P].rearrange("p (a i) -> p a i", a=2)[:, :, 0:n],
                                     ACT.Exp, scale=-1.0).then_inc(ecum_ready, 1)

            def z_silu(k, j):
                need(act, z_ps, passed(k, J, j))
                need(act, g_ready, passed(back(k, 2), J, j))
                nc.scalar.activation(sz[k[1]][:, j, :], pA[1][:], ACT.Silu).then_inc(sz_ready, 1)

            def x_token(k, j):
                before = passed(back(k, 1), J, j)
                need(act, xT_ps, passed(k, J, j))
                need(act, xdt_ready, before)
                need(act, xd_ready, before)
                nc.scalar.copy(xtok[j][:], pT[:]).then_inc(xtok_ready, 1)

            def b_and_g(k, j):
                s = k[1]
                need(act, g_ps, passed(k, J, j))
                need(act, gm_ready, passed(back(k, 1), J, j))
                need(act, state_ps, 3 * k[0] + (-1 if (s, j) == (0, 1) else s + j))
                nc.scalar.copy(bg[j][:].rearrange("p a t -> p (a t)"), pG[:, 0:2 * P]).then_inc(bg_ready, 1)

            def decay(k, j):
                s = k[1]
                act.wait_ge(r_ld[s], 16 * (k[0] + 1))
                act.wait_ge(cum_ready, passed(k, 1, 0))
                for h in range(NH):
                    last = nc.scalar.activation(R[s][:, j, h, :], R[s][:, j, h, :], ACT.Relu,
                                                bias=cum[s][:, j, h:h + 1])
                last.then_inc(diff_ready, 1)

            def decay_exp(k, j):
                act.wait_ge(diff_ready, passed(k, J, j))
                nc.scalar.activation(R[k[1]][:, j], R[k[1]][:, j], ACT.Exp, scale=-1.0).then_inc(exp_ready, 1)

            def gate_square(k, j):
                need(act, g_ready, passed(k, J, j))
                need(act, ss_ready, passed(k, J, j + -1))
                nc.scalar.activation(sqj[:], g[j][:], ACT.Square, accum_out=ss[:, j:j + 1]).then_inc(ss_ready, 1)

            def gate_hi(k, j):
                need(act, gT_ps, passed(k, J, j))
                need(act, proj_ps, passed(back(k, 1), J, j))
                nc.scalar.copy(gTh[j][:], pT[:].rearrange("p (c t) -> p c t", c=KI)).then_inc(gTh_ready, 1)

            def u2_hi(k, j):
                need(act, u2T_ps, passed(k, J, j))
                need(act, up_ps, passed(back(k, 2), 4, 3))
                nc.scalar.copy(u2Th[k[1]][:, :, j * P:(j + 1) * P],
                               pG[:, 0:DM].rearrange("p (c t) -> p c t", c=KM)).then_inc(u2Th_ready, 1)

            def gelu(k, q):
                need(act, up_ps, passed(k, 4, q))
                need(act, hl_ready, passed(k if q >= 2 else back(k, 1), 4, (q + 2) % 4))
                for c in range(2):
                    nc.scalar.activation(hf[q % 2][:, c, :], pF[q % 2][:, c * HALF:(c + 1) * HALF], ACT.Gelu,
                                         bias=b1s[:, 2 * q + c:2 * q + c + 1]).then_inc(gelu_ready, 1)

            def hidden_hi(k, q):
                act.wait_ge(gelu_ready, passed(k, KF, 2 * q + 1))
                need(act, down_ps, passed(back(k, 1), J, J - 1))
                nc.scalar.copy(hh[:, 2 * q:2 * q + 2, :], hf[q % 2][:]).then_inc(hh_ready, 1)

            run(act, {"u hi": uT_hi, "dt rows": dt_out, "conv first": conv_first_tap, "conv silu": silu,
                      "dt token": dt_token, "softplus exp": softplus_exp, "sums head": sums_head,
                      "sums token": sums_token, "z silu": z_silu, "x token": x_token, "B and G": b_and_g,
                      "decay": decay, "decay exp": decay_exp, "gate square": gate_square, "gate hi": gate_hi, "u2 hi": u2_hi,
                      "gelu": gelu, "hidden hi": hidden_hi})

        @block.tensor
        def _(pe):
            pe.wait_ge(absum_ready, 2)
            pe.wait_ge(consts, CONSTS)
            nc.tensor.matmul(pG[:, 0:2], ones[:], absum[:], start=True, stop=True).then_inc(absum_ps, 1)
            pe.wait_ge(weights_ready, 1)

            def transpose(dst, src):
                return nc.tensor.matmul(dst, src, ident[:], is_transpose=True, start=True, stop=True)

            def uT(k, _):
                s = k[1]
                need(pe, u_ready, passed(k, J, J - 1))
                need(pe, conv_done, passed(back(k, 1), CH, 4))
                for c in range(KM):
                    for j in range(J):
                        last = transpose(pA[0][:, c * HALF + j * P:c * HALF + (j + 1) * P],
                                         XU[s][:, j, 1, c * P:(c + 1) * P])
                last.then_inc(uT_ps, 1)

            def dt(k, _):
                s = k[1]
                need(pe, uTl_ready, passed(k, 1, 0))
                need(pe, conv_done, passed(back(k, 1), CH, 5))
                for c in range(KM):
                    for n, uT_part in enumerate((uTh, uTl)):
                        last = nc.tensor.matmul(pA[1][:, 0:HALF], wdt[:, c, :], uT_part[s][:, c, CARRY:UW],
                                                start=(c, n) == (0, 0), stop=(c, n) == (KM - 1, 1))
                last.then_inc(dt_ps, 1)

            def conv_in(k, q):
                s = k[1]
                for i in range(2):
                    m = 2 * q + i
                    if i == 0:
                        need(pe, (uTl_ready, dtt_ready, ecum_ready)[q], passed(k, 1, 0))
                    elif q == 0:
                        need(pe, dtr_ready, passed(k, 1, 0))
                    else:
                        need(pe, sz_ready, passed(k, J, q - 1))
                    cols = slice(DI + m * P, DI + (m + 1) * P)
                    for c in range(KM):
                        for n, (w, uT_part) in enumerate(((win_hi, uTh), (win_hi, uTl), (win_lo, uTh))):
                            last = nc.tensor.matmul(pA[i][:, 0:UW], w[:, c, cols], uT_part[s][:, c, :],
                                                    start=(c, n) == (0, 0), stop=(c, n) == (KM - 1, 2))
                    last.then_inc(conv_ps, 1)

            def dtT(k, _):
                need(pe, dtr_ready, passed(k, 1, 0))
                need(pe, conv_done, passed(k, CH, 0))
                for j in range(J):
                    last = transpose(pA[0][:, j * P:(j + 1) * P], dtr[:, j * P:(j + 1) * P])
                last.then_inc(dtT_ps, 1)

            def sums(k, _):
                need(pe, dA_ready, passed(k, 1, 0))
                need(pe, conv_done, passed(k, CH, 2))
                nc.tensor.matmul(pA[0][:, 0:2 * P], dA[:], tri[:].rearrange("p a i -> p (a i)"),
                                 start=True, stop=True).then_inc(cum_ps, 1)

            def sumsT(k, _):
                need(pe, cr_ready, passed(k, 1, 0))
                for a in range(2):
                    last = transpose(pA[0][:, a * P:(a + 1) * P], cr[:, a, :])
                last.then_inc(cumT_ps, 1)

            def z(k, j):
                s = k[1]
                need(pe, conv_done, passed(k, CH, 2 * j + 1))
                for c in range(KM):
                    for n, (uT_part, w) in enumerate(((uTh, win_hi), (uTh, win_lo), (uTl, win_hi))):
                        last = nc.tensor.matmul(pA[1][:], uT_part[s][:, c, CARRY + j * P:CARRY + (j + 1) * P],
                                                w[:, c, 0:DI], start=(c, n) == (0, 0), stop=(c, n) == (KM - 1, 2))
                last.then_inc(z_ps, 1)

            def x_and_g(k, j):
                s = k[1]
                cols = slice(j * P, (j + 1) * P)
                need(pe, xbc_ready, passed(k, 3, 2))
                if j == 0:
                    need(pe, gTl_ready, passed(back(k, 1), J, 1))
                else:
                    need(pe, xtok_ready, passed(k, J, 0))
                for m in range(XS):
                    last = transpose(pT[:, m * P:(m + 1) * P], xbc[s][:, m, cols])
                last.then_inc(xT_ps, 1)
                if j == 1:
                    need(pe, bg_ready, passed(k, J, 0))
                need(pe, u2Tl_ready, passed(back(k, 1), J, j))
                transpose(pG[:, 0:P], xbc[s][:, XS, cols])
                nc.tensor.matmul(pG[:, P:2 * P], xbc[s][:, XS, cols], xbc[s][:, XS + 1, cols],
                                 start=True, stop=True).then_inc(g_ps, 1)

            def tile_before(k, j):
                return passed(k if j else back(k, 1), J, 1 - j)

            def inter(k, j):
                if not first_tile(k, j):
                    need(pe, s_ready, state_count(k, j) + -1)
                    need(pe, y_ready, tile_before(k, j))
                    nc.tensor.matmul(pY[:], xbc[k[1]][:, XS + 1, j * P:(j + 1) * P], S[:],
                                     start=True, stop=True).then_inc(inter_ps, 1)

            def intra(k, j):
                s = k[1]
                if first_tile(k, j):
                    need(pe, y_ready, tile_before(k, j))
                else:
                    need(pe, t1_ready, inter_count(k, j))
                need(pe, mix_ready, passed(k, J, j))
                need(pe, xdt_ready, passed(k, J, j))
                for h in range(NH):
                    last = nc.tensor.matmul(pY[:, h * HD:(h + 1) * HD], R[s][:, j, h, :], xdt[j][:, h * HD:(h + 1) * HD],
                                            start=True, stop=True)
                last.then_inc(intra_ps, 1)

            def gateT(k, j):
                need(pe, g_ready, passed(k, J, j))
                if j == 0:
                    need(pe, xtok_ready, passed(k, J, 1))
                else:
                    need(pe, gTl_ready, passed(k, J, 0))
                for c in range(KI):
                    last = transpose(pT[:, c * P:(c + 1) * P], g[j][:, c * P:(c + 1) * P])
                last.then_inc(gT_ps, 1)

            def project(k, j):
                need(pe, gTl_ready, passed(k, J, j))
                if last_tile(k, j):
                    need(pe, r_ready, passed(k, J, 0))
                else:
                    need(pe, s_ready, state_count(k, j))
                for c in range(KI):
                    for n, (gT_part, w) in enumerate(((gTh, wout_hi), (gTh, wout_lo), (gTl, wout_hi))):
                        last = nc.tensor.matmul(pS[:, 0:DM], gT_part[j][:, c, :], w[:, c, :],
                                                start=(c, n) == (0, 0), stop=(c, n) == (KI - 1, 2))
                last.then_inc(proj_ps, 1)

            def state(k, j):
                if not last_tile(k, j):
                    need(pe, xst_ready, state_count(k, j))
                    need(pe, bg_ready, passed(k, J, j))
                    need(pe, r_ready, tile_before(k, j))
                    nc.tensor.matmul(pS[:], bg[j][:, 0, :], xst[j][:], start=True, stop=True).then_inc(state_ps, 1)

            def u2T(k, j):
                need(pe, u2_ready, passed(k, J, j))
                if j == 0 or final(k):
                    need(pe, bg_ready, passed(k, J, 1))
                else:
                    need(pe, bg_ready, passed(back(k, -1), J, 0))
                if final(k) and j == 1:
                    need(pe, u2Tl_ready, passed(k, J, 0))
                for c in range(KM):
                    last = transpose(pG[:, c * P:(c + 1) * P], u2[j][:, c * P:(c + 1) * P])
                last.then_inc(u2T_ps, 1)

            def up(k, q):
                s = k[1]
                need(pe, u2Tl_ready, passed(k, J, J - 1))
                if q < 2:
                    need(pe, ffo_ready, passed(back(k, 1), J, q))
                else:
                    need(pe, gelu_ready, passed(k, KF, 2 * (q - 2) + 1))
                for i in range(2):
                    m = 2 * q + i
                    for c in range(KM):
                        for n, part in enumerate((u2Th, u2Tl)):
                            last = nc.tensor.matmul(pF[q % 2][:, i * HALF:(i + 1) * HALF],
                                                    w1_t[:, c * FF + m * P:c * FF + (m + 1) * P], part[s][:, c, :],
                                                    start=(c, n) == (0, 0), stop=(c, n) == (KM - 1, 1))
                last.then_inc(up_ps, 1)

            def down(k, j):
                need(pe, hl_ready, passed(k, 4, 3))
                need(pe, gelu_ready, passed(k, KF, 5 + 2 * j))
                for c in range(KF):
                    for n, part in enumerate((hh, hl)):
                        last = nc.tensor.matmul(pF[j][:, 0:DM], part[:, c, j * P:(j + 1) * P],
                                                w2_t[:, c * DM:(c + 1) * DM],
                                                start=(c, n) == (0, 0), stop=(c, n) == (KF - 1, 1))
                last.then_inc(down_ps, 1)

            run(pe, {"uT": uT, "dt": dt, "conv": conv_in, "dtT": dtT, "sums": sums, "sumsT": sumsT, "z": z,
                     "xT and G": x_and_g, "inter": inter, "intra": intra, "gateT": gateT,
                     "project": project, "state": state, "u2T": u2T, "up": up, "down": down})


def kernel(L0_attn_x, L0_attn_in_proj_w, L0_attn_conv_w, L0_attn_conv_b, L0_attn_dt_bias, L0_attn_A_log,
           L0_attn_D, L0_attn_norm_w, L0_attn_out_proj_w, L0_ffn_W1, L0_ffn_b1, L0_ffn_W2, L0_ffn_b2):
    import concourse.bacc as bacc
    from concourse.bass_utils import run_bass_kernel_spmd

    def by_partition(a):
        a = np.asarray(a)
        return np.moveaxis(a.reshape(a.shape[0] // P, P, *a.shape[1:]), 0, 1)

    arrays = {
        "x": L0_attn_x, "w_in": np.asarray(L0_attn_in_proj_w).T,
        "conv_w": by_partition(L0_attn_conv_w), "conv_b": by_partition(L0_attn_conv_b),
        "dt_bias": L0_attn_dt_bias, "a_log": L0_attn_A_log, "d_skip": L0_attn_D,
        "norm_w": by_partition(L0_attn_norm_w), "w_out": np.asarray(L0_attn_out_proj_w).T,
        "w1": np.asarray(L0_ffn_W1).T, "b1": by_partition(L0_ffn_b1),
        "w2": np.asarray(L0_ffn_W2).T, "b2": L0_ffn_b2,
    }
    arrays = {n: np.ascontiguousarray(a) for n, a in arrays.items()}
    nc = bacc.Bacc("TRN2", target_bir_lowering=False, num_devices=1)
    aps = [nc.dram_tensor(n, a.shape, mybir.dt.from_np(a.dtype), kind="ExternalInput").ap()
           for n, a in arrays.items()]
    heads = arrays["dt_bias"].shape[0]
    cum_dram = nc.dram_tensor("cum_dram", (2, 2 * heads, P), F32, kind="Internal").ap()
    out = nc.dram_tensor("out", arrays["x"].shape, F32, kind="ExternalOutput").ap()
    build(nc, *aps, cum_dram, out)
    r = run_bass_kernel_spmd(nc, [arrays], core_ids=[0])
    return r.results[0]["out"]
```

```python
from contextlib import ExitStack

import numpy as np
import concourse.bass as bass
from concourse import mybir

F32 = mybir.dt.float32
F32R = mybir.dt.float32r
ALU = mybir.AluOpType
ACT = mybir.ActivationFunctionType
AX = mybir.AxisListType

P = 128
CONSTS = 16
SP_STEPS = 15
CARRY = 4
EPS = 1e-5

STEP = [
    ("ln1 stats", 0, 1), ("gate rsqrt", 0, 3), ("attn out", 0, 3), ("ln1 eps", 0, 1), ("attn stats", 0, 3),
    ("add inter", 1, 3), ("intra", 1, 3), ("scale state", 1, 3), ("attn eps", 0, 3), ("gelu", 0, 4),
    ("ln1 rsqrt", 0, 1), ("hidden hi", 0, 4), ("store", 0, 6), ("conv", 2, 2), ("up", 1, 4), ("u", 0, 1),
    ("y", 1, 3), ("conv first", 2, 2), ("state", 1, 3), ("add ffn", 0, 5), ("gelu", 1, 4), ("hidden hi", 1, 4),
    ("attn rsqrt", 0, 3), ("attn norm", 0, 3), ("up", 2, 4), ("hidden lo", 0, 4), ("gelu", 2, 4),
    ("gate", 1, 3), ("gateT", 1, 3), ("gate hi", 1, 3), ("hidden lo", 1, 4), ("add residual", 0, 3),
    ("up", 3, 4), ("conv taps", 2, 2), ("uT", 0, 1), ("new state", 1, 3), ("hidden hi", 2, 4),
    ("gate lo", 1, 3), ("u hi", 0, 1), ("gelu", 3, 4), ("ln2 stats", 0, 3), ("u lo", 0, 1), ("hidden lo", 2, 4),
    ("ln2 eps", 0, 3), ("sums back", 0, 2), ("ln2 rsqrt", 0, 3), ("store", 1, 6), ("gate square", 1, 3),
    ("hidden hi", 3, 4), ("project", 1, 3), ("dt", 0, 1), ("dt decay", 0, 2), ("dt rows", 0, 1),
    ("gate mean", 1, 3), ("gate rsqrt", 1, 3), ("conv silu", 2, 2), ("u2", 0, 3), ("u2T", 0, 3),
    ("hidden lo", 3, 4), ("u2 hi", 0, 3), ("conv", 0, 1), ("conv first", 0, 1), ("attn out", 1, 3),
    ("down", 0, 4), ("attn stats", 1, 3), ("attn eps", 1, 3), ("attn rsqrt", 1, 3), ("decay", 0, 2),
    ("u2 lo", 0, 3), ("xT and G", 0, 2), ("inter", 0, 2), ("attn norm", 1, 3), ("B and G", 0, 2),
    ("conv taps", 0, 1), ("dtT", 0, 1), ("add ffn", 1, 5), ("add residual", 1, 3), ("ln2 stats", 1, 3),
    ("dt token", 0, 1), ("x token", 0, 2), ("conv silu", 0, 1), ("keep xu", 0, 2), ("keep xu", 1, 2),
    ("ln2 eps", 1, 3), ("ln2 rsqrt", 1, 3), ("ffn stats", 0, 4), ("x for state", 0, 2), ("softplus", 0, 1),
    ("ffn eps", 0, 4), ("softplus", 1, 1), ("z", 0, 1), ("u2", 1, 3), ("z silu", 0, 1), ("softplus", 2, 1),
    ("scale state", 0, 2), ("x dt", 0, 2), ("softplus exp", 0, 1), ("inter decay", 0, 2), ("softplus", 3, 1),
    ("mask", 0, 2), ("skip", 0, 2), ("softplus", 4, 1), ("down", 1, 4), ("ffn stats", 1, 4),
    ("decay exp", 0, 2), ("softplus", 5, 1), ("softplus", 6, 1), ("u2T", 1, 3), ("u2 hi", 1, 3), ("conv", 1, 1),
    ("softplus", 7, 1), ("ffn eps", 1, 4), ("load x", 0, 0), ("mix", 0, 2), ("conv first", 1, 1),
    ("u2 lo", 1, 3), ("ffn rsqrt", 0, 4), ("state", 0, 2), ("decay", 1, 2), ("softplus", 8, 1),
    ("softplus", 9, 1), ("add inter", 0, 2), ("xT and G", 1, 2), ("x token", 1, 2), ("intra", 0, 2),
    ("B and G", 1, 2), ("decay exp", 1, 2), ("conv taps", 1, 1), ("ffn rsqrt", 1, 4), ("softplus", 10, 1),
    ("ffn norm", 0, 4), ("softplus", 11, 1), ("z", 1, 1), ("x for state", 1, 2), ("softplus", 12, 1),
    ("y", 0, 2), ("softplus", 13, 1), ("up", 0, 3), ("gate", 0, 2), ("gateT", 0, 2), ("conv silu", 1, 1),
    ("gate hi", 0, 2), ("softplus", 14, 1), ("ffn norm", 1, 4), ("softplus", 15, 1), ("sums", 0, 1),
    ("mask", 1, 2), ("skip", 1, 2), ("mix", 1, 2), ("new state", 0, 2), ("inter", 1, 2), ("sums head", 0, 1),
    ("sumsT", 0, 1), ("x dt", 1, 2), ("gate lo", 0, 2), ("gate square", 0, 2), ("z silu", 1, 1),
    ("inter decay", 1, 2), ("sums token", 0, 1), ("gate mean", 0, 2), ("project", 0, 2), ("sums out", 0, 1),
]
LAG = max(lag for _, _, lag in STEP)


def build(nc, x, w_in, conv_w, conv_b, dt_bias, a_log, d_skip, norm_w, w_out, w1, b1, w2, b2,
          cum_dram, out):
    B, L, DM = x.shape
    KM = DM // P
    DIN = w_in.shape[1]
    DI = w_out.shape[0]
    KI = DI // P
    NH = dt_bias.shape[0]
    HD = DI // NH
    CH = conv_w.shape[1]
    TAPS = conv_w.shape[2]
    XS = KI
    FF = w1.shape[1]
    KF = FF // P
    HALF = L // 2
    J = HALF // P
    UW = CARRY + HALF
    assert (KM, KI, CH, J, KF, TAPS, L // HALF) == (2, 4, 6, 2, 8, 4, 2)

    xv = x.rearrange("b (s j p) d -> b s p j d", s=2, p=P)
    ov = out.rearrange("b (s j p) d -> b s j p d", s=2, p=P)

    with ExitStack() as ctx:
        def sb(name, shape, dt=F32):
            return ctx.enter_context(nc.sbuf_tensor(name, shape, dt))

        def bank(name):
            return ctx.enter_context(nc.psum_tensor(name, [P, 512], F32))

        def sem(name):
            return ctx.enter_context(nc.semaphore(name))

        win_f = sb("win_f", [P, KM, DIN])
        win_hi = sb("win_hi", [P, KM, DIN], F32R)
        win_lo = sb("win_lo", [P, KM, DIN], F32R)
        wdt = sb("wdt", [P, KM, P], F32R)
        wout_hi = sb("wout_hi", [P, KI, DM], F32R)
        wout_lo = sb("wout_lo", [P, KI, DM], F32R)
        w1_t = sb("w1_t", [P, KM * FF], F32R)
        w2_t = sb("w2_t", [P, KF * DM], F32R)
        convw = sb("convw", [P, CH, TAPS])
        convb = sb("convb", [P, CH])
        b1s = sb("b1s", [P, KF])
        nws = sb("nws", [P, KI])
        b2s = sb("b2s", [P, DM])
        b2r = sb("b2r", [P, DM], F32R)
        ones_r = sb("ones_r", [P, P], F32R)
        dtb = sb("dtb", [P, NH])
        a_pos = sb("a_pos", [P, NH])
        dsk = sb("dsk", [P, NH])
        ident = sb("ident", [P, P])
        tri = sb("tri", [P, 2, P])
        upper, lower = tri[:, 0, :], tri[:, 1, :]
        ones = sb("ones", [P, P])
        mhalf = sb("mhalf", [P, J])
        absum = sb("absum", [P, 2])
        thr = sb("thr", [P, 2])
        nthr = sb("nthr", [P, 2])
        XU = [sb(f"XU{s}", [P, J, 2, DM]) for s in range(2)]
        XR = [sb(f"XR{j}", [P, 2, DM]) for j in range(J)]
        st1 = sb("st1", [P, J, 6])
        mv1 = sb("mv1", [P, J, 2])
        ve1 = sb("ve1", [P, J])
        rs1 = sb("rs1", [P, J])
        uTh = [sb(f"uTh{s}", [P, KM, UW], F32R) for s in range(2)]
        uTl = [sb(f"uTl{s}", [P, KM, UW], F32R) for s in range(2)]
        acc = [sb(f"acc{q}", [P, 2, HALF]) for q in range(2)]
        xbc = [sb(f"xbc{s}", [P, CH, HALF]) for s in range(2)]
        sz = [sb(f"sz{s}", [P, J, DI]) for s in range(2)]
        dtr = sb("dtr", [P, HALF])
        dtt = sb("dtt", [P, J, 2 * NH])
        sp = sb("sp", [P, 8, J, NH])
        dts = [sb(f"dts{s}", [P, J, NH]) for s in range(2)]
        dA = sb("dA", [P, P])
        cr = sb("cr", [P, 2, P])
        cum = [sb(f"cum{s}", [P, J, NH]) for s in range(2)]
        ecum = [sb(f"ecum{s}", [P, 2, J, NH]) for s in range(2)]
        etot = [sb(f"etot{s}", [P, J, NH]) for s in range(2)]
        dtdec = [sb(f"dtdec{s}", [P, J, NH]) for s in range(2)]
        R = [sb(f"R{s}", [P, J, NH, P]) for s in range(2)]
        xtok = [sb(f"xtok{j}", [P, DI]) for j in range(J)]
        bg = [sb(f"bg{j}", [P, 2, P]) for j in range(J)]
        gm = [sb(f"gm{j}", [P, P]) for j in range(J)]
        xdt = [sb(f"xdt{j}", [P, DI]) for j in range(J)]
        xst = [sb(f"xst{j}", [P, DI]) for j in range(J)]
        xd = [sb(f"xd{j}", [P, DI]) for j in range(J)]
        t1 = [sb(f"t1{j}", [P, DI]) for j in range(J)]
        g = [sb(f"g{j}", [P, DI]) for j in range(J)]
        S = sb("S", [P, DI])
        sqj = sb("sqj", [P, DI])
        ss = sb("ss", [P, J])
        vg = sb("vg", [P, J])
        rg = sb("rg", [P, J])
        gTh = [sb(f"gTh{j}", [P, KI, P], F32R) for j in range(J)]
        gTl = [sb(f"gTl{j}", [P, KI, P], F32R) for j in range(J)]
        r = [sb(f"r{j}", [P, DM]) for j in range(J)]
        sta = sb("sta", [P, J, 6])
        mva = sb("mva", [P, J, 2])
        vea = sb("vea", [P, J])
        rsa = sb("rsa", [P, J])
        x1 = [sb(f"x1{s}", [P, J, DM]) for s in range(2)]
        st2 = sb("st2", [P, J, 6])
        mv2 = sb("mv2", [P, J, 2])
        ve2 = sb("ve2", [P, J])
        rs2 = sb("rs2", [P, J])
        u2 = [sb(f"u2{j}", [P, DM]) for j in range(J)]
        u2Th = [sb(f"u2Th{s}", [P, KM, HALF], F32R) for s in range(2)]
        u2Tl = [sb(f"u2Tl{s}", [P, KM, HALF], F32R) for s in range(2)]
        hf = [sb(f"hf{q}", [P, 2, HALF]) for q in range(2)]
        hh = sb("hh", [P, KF, HALF], F32R)
        hl = sb("hl", [P, KF, HALF], F32R)
        ffo = [sb(f"ffo{j}", [P, DM]) for j in range(J)]
        stf = sb("stf", [P, J, 6])
        mvf = sb("mvf", [P, J, 2])
        vef = sb("vef", [P, J])
        rsf = sb("rsf", [P, J])
        ob = [sb(f"ob{j}", [P, DM]) for j in range(J)]

        wout_f = xbc[0][:].rearrange("p c t -> p (c t)")[:, 0:KI * DM].rearrange("p (c n) -> p c n", c=KI)
        w1_f = R[0][:].rearrange("p j h i -> p (j h i)")
        w2_f = R[1][:].rearrange("p j h i -> p (j h i)")

        pA = [bank(f"pA{i}") for i in range(2)]
        pT = bank("pT")
        pG = bank("pG")
        pY = bank("pY")
        pS = bank("pS")
        pF = [bank(f"pF{i}") for i in range(2)]

        w_ld = {n: sem(f"{n}_ld") for n in ("win", "wout", "w1", "w2", "small")}
        x_ld = [sem(f"x_ld{s}") for s in range(2)]
        xr_ld = [sem(f"xr_ld{j}") for j in range(J)]
        cum_st = sem("cum_st")
        r_ld = [sem(f"r_ld{s}") for s in range(2)]
        out_st = [sem(f"out_st{j}") for j in range(J)]
        consts = sem("consts")
        prep = sem("prep")
        absum_ready = sem("absum_ready")
        absum_ps = sem("absum_ps")
        ready = {n: sem(f"{n}_ready") for n in ("win", "wout", "w1", "w2")}
        a_exp = sem("a_exp")
        ln1_mv = sem("ln1_mv")
        ln1_ve = sem("ln1_ve")
        ln1_rstd = sem("ln1_rstd")
        u_ready = sem("u_ready")
        uT_ps = sem("uT_ps")
        uTh_ready = sem("uTh_ready")
        uTl_ready = sem("uTl_ready")
        dt_ps = sem("dt_ps")
        dtr_ready = sem("dtr_ready")
        conv_ps = sem("conv_ps")
        conv_first = sem("conv_first")
        conv_tap = sem("conv_tap")
        conv_done = sem("conv_done")
        xbc_ready = sem("xbc_ready")
        dtT_ps = sem("dtT_ps")
        dtt_ready = sem("dtt_ready")
        sp_step = sem("sp_step")
        sp_exp = sem("sp_exp")
        dA_ready = sem("dA_ready")
        cum_ps = sem("cum_ps")
        cum_ready = sem("cum_ready")
        ecum_ready = sem("ecum_ready")
        etot_ready = sem("etot_ready")
        dtdec_ready = sem("dtdec_ready")
        cumT_ps = sem("cumT_ps")
        cr_ready = sem("cr_ready")
        z_ps = sem("z_ps")
        sz_ready = sem("sz_ready")
        xT_ps = sem("xT_ps")
        g_ps = sem("g_ps")
        xtok_ready = sem("xtok_ready")
        bg_ready = sem("bg_ready")
        gm_ready = sem("gm_ready")
        xdt_ready = sem("xdt_ready")
        xst_ready = sem("xst_ready")
        xd_ready = sem("xd_ready")
        diff_ready = sem("diff_ready")
        exp_ready = sem("exp_ready")
        mix_ready = sem("mix_ready")
        inter_ps = sem("inter_ps")
        t1_ready = sem("t1_ready")
        yx_ready = sem("yx_ready")
        intra_ps = sem("intra_ps")
        y_ready = sem("y_ready")
        g_ready = sem("g_ready")
        ss_ready = sem("ss_ready")
        vg_ready = sem("vg_ready")
        rg_ready = sem("rg_ready")
        gT_ps = sem("gT_ps")
        gTh_ready = sem("gTh_ready")
        gTl_ready = sem("gTl_ready")
        proj_ps = sem("proj_ps")
        r_ready = sem("r_ready")
        state_ps = sem("state_ps")
        s_scaled = sem("s_scaled")
        s_ready = sem("s_ready")
        lna_mv = sem("lna_mv")
        lna_ve = sem("lna_ve")
        lna_rstd = sem("lna_rstd")
        rn_ready = sem("rn_ready")
        x1_ready = sem("x1_ready")
        ln2_mv = sem("ln2_mv")
        ln2_ve = sem("ln2_ve")
        ln2_rstd = sem("ln2_rstd")
        u2_ready = sem("u2_ready")
        u2T_ps = sem("u2T_ps")
        u2Th_ready = sem("u2Th_ready")
        u2Tl_ready = sem("u2Tl_ready")
        up_ps = sem("up_ps")
        gelu_ready = sem("gelu_ready")
        hh_ready = sem("hh_ready")
        hl_ready = sem("hl_ready")
        down_ps = sem("down_ps")
        lnf_mv = sem("lnf_mv")
        lnf_ve = sem("lnf_ve")
        lnf_rstd = sem("lnf_rstd")
        fn_ready = sem("fn_ready")
        ob_ready = sem("ob_ready")

        def passed(k, n, i):
            return k[0] * (2 * n) + (k[1] * n + i + 1)

        def need(eng, s, count):
            if not isinstance(count, int) or count > 0:
                eng.wait_ge(s, count)

        def back(k, n):
            h = k[1] - n
            return (k[0] + h // 2, h % 2)

        def first_tile(k, j):
            return (k[1], j) == (0, 0)

        def last_tile(k, j):
            return (k[1], j) == (1, J - 1)

        def inter_count(k, j):
            return 3 * k[0] + 2 * k[1] + j

        def state_count(k, j):
            return 3 * k[0] + 2 * k[1] + j + 1

        def half(t):
            return (t // 2, t % 2)

        def is_half(k, n):
            return isinstance(k[0], int) and k[0] * 2 + k[1] == n

        def run(eng, parts):
            def step(k, check=None):
                for part, arg, lag in STEP:
                    if part in parts and (check is None or 0 <= check - lag < 2 * B):
                        parts[part](back(k, lag), arg)

            first = LAG // 2 + 2
            for t in range(2 * first):
                step(half(t), t)
            with eng.Fori(first, B) as b:
                step((b, 0))
                step((b, 1))
            for t in range(2 * B, 2 * B + LAG):
                step(half(t), t)

        block = ctx.enter_context(nc.Block())

        @block.sync
        def _(sy):
            sy.dma_start(win_f[:], w_in.rearrange("(c p) n -> p c n", p=P)).then_inc(w_ld["win"], 16)

            def load_x(k, _):
                for j in range(J):
                    need(sy, xr_ld[j], passed(back(k, 2), 16, 15))
                sy.dma_start(XU[k[1]][:, :, 0, :], xv[k[0], k[1]]).then_inc(x_ld[k[1]], 16)

            def keep_xu(k, j):
                need(sy, x1_ready, passed(back(k, 1), J, j))
                sy.dma_start(XR[j][:], XU[k[1]][:, j]).then_inc(xr_ld[j], 16)

            def sums_out(k, _):
                need(sy, cr_ready, passed(k, 1, 0))
                sy.dma_start(cum_dram[k[1]], cr[0:J * NH, 0, :]).then_inc(cum_st, 16)

            def sums_back(k, _):
                sy.wait_ge(cum_st, passed(k, 16, 15))
                need(sy, intra_ps, passed(back(k, 2), J, J - 1))
                for n, name in enumerate(("w1", "w2")):
                    if is_half(k, n):
                        sy.wait_ge(ready[name], 1)
                sy.dma_start(R[k[1]][:].rearrange("p j h i -> p (j h i)"),
                             cum_dram[k[1]].rearrange("a i -> (a i)").partition_broadcast(P)
                             ).then_inc(r_ld[k[1]], 16)

            def store(k, j):
                need(sy, ob_ready, passed(k, J, j))
                sy.dma_start(ov[k[0], k[1], j], ob[j][:]).then_inc(out_st[j], 16)

            run(sy, {"load x": load_x, "keep xu": keep_xu, "sums out": sums_out, "sums back": sums_back,
                     "store": store})
            for j in range(J):
                sy.wait_ge(out_st[j], 16 * 2 * B)

        @block.gpsimd
        def _(pool):
            nc.gpsimd.memset(ident[:], 0.0).then_inc(consts, 1)
            nc.gpsimd.memset(upper, 1.0).then_inc(consts, 1)
            nc.gpsimd.memset(lower, 1.0).then_inc(consts, 1)
            nc.gpsimd.memset(ones[:], 1.0).then_inc(consts, 1)
            nc.gpsimd.memset(mhalf[:], -0.5).then_inc(consts, 1)
            for s in range(2):
                nc.gpsimd.memset(uTh[s][:, :, 0:CARRY].bitcast(F32), 0.0).then_inc(consts, 1)
                nc.gpsimd.memset(uTl[s][:, :, 0:CARRY].bitcast(F32), 0.0).then_inc(consts, 1)
            nc.gpsimd.memset(wdt[:].bitcast(F32), 0.0).then_inc(consts, 1)
            nc.gpsimd.memset(dA[:], 0.0).then_inc(consts, 1)
            nc.gpsimd.memset(b2r[:].bitcast(F32), 0.0).then_inc(consts, 1)
            nc.gpsimd.memset(ones_r[:].bitcast(F32), 1.0).then_inc(consts, 1)
            pool.wait_ge(consts, 5)
            nc.gpsimd.affine_select(out=ident[:], in_=ident[:], compare_op=ALU.not_equal, fill=1.0,
                                    base=0, pattern=[[-1, P]], channel_multiplier=1).then_inc(consts, 1)
            nc.gpsimd.affine_select(out=upper, in_=upper, compare_op=ALU.is_ge, fill=0.0,
                                    base=0, pattern=[[1, P]], channel_multiplier=-1).then_inc(consts, 1)
            nc.gpsimd.affine_select(out=lower, in_=lower, compare_op=ALU.is_ge, fill=0.0,
                                    base=-1, pattern=[[-1, P]], channel_multiplier=1).then_inc(consts, 1)
            pool.wait_ge(consts, CONSTS)

            def rstd(ve_ready, rstd_ready, ve, rs, k, n, i, cols):
                need(pool, ve_ready, passed(k, n, i))
                nc.gpsimd.tensor_tensor(rs[:, cols], ve[:, cols], mhalf[:, 0:cols.stop - cols.start],
                                        ALU.pow).then_inc(rstd_ready, 1)

            def ln1_rsqrt(k, _):
                need(pool, u_ready, passed(back(k, 1), J, J - 1))
                rstd(ln1_ve, ln1_rstd, ve1, rs1, k, 1, 0, slice(0, J))

            def mask(k, j):
                need(pool, bg_ready, passed(k, J, j))
                need(pool, mix_ready, passed(back(k, 1), J, j))
                nc.gpsimd.tensor_tensor(gm[j][:], bg[j][:, 1, :], upper, ALU.mult).then_inc(gm_ready, 1)

            def by_head(ap):
                return ap.rearrange("p (h d) -> p h d", h=NH)

            def x_for_state(k, j):
                b, s = k
                if not last_tile(k, j):
                    need(pool, xtok_ready, passed(k, J, j))
                    need(pool, dtdec_ready, passed(k, 1, 0))
                    need(pool, state_ps, 3 * b + (-1 if (s, j) == (0, 1) else s))
                    nc.gpsimd.tensor_tensor(by_head(xst[j][:]), by_head(xtok[j][:]),
                                            dtdec[s][:, j, :].unsqueeze(2).to_broadcast([P, NH, HD]),
                                            ALU.mult).then_inc(xst_ready, 1)

            def skip_term(k, j):
                need(pool, xtok_ready, passed(k, J, j))
                need(pool, y_ready, passed(back(k, 1), J, j))
                nc.gpsimd.tensor_tensor(by_head(xd[j][:]), by_head(xtok[j][:]),
                                        dsk[:].unsqueeze(2).to_broadcast([P, NH, HD]),
                                        ALU.mult).then_inc(xd_ready, 1)

            def mix(k, j):
                need(pool, exp_ready, passed(k, J, j))
                pool.wait_ge(gm_ready, passed(k, J, j))
                nc.gpsimd.tensor_tensor(R[k[1]][:, j], R[k[1]][:, j],
                                        gm[j][:].unsqueeze(1).to_broadcast([P, NH, P]),
                                        ALU.mult).then_inc(mix_ready, 1)

            def add_inter(k, j):
                if not first_tile(k, j):
                    need(pool, t1_ready, inter_count(k, j))
                    pool.wait_ge(xd_ready, passed(k, J, j))
                    nc.gpsimd.tensor_tensor(xd[j][:], t1[j][:], xd[j][:], ALU.add).then_inc(yx_ready, 1)

            def gate_rsqrt(k, j):
                rstd(vg_ready, rg_ready, vg, rg, k, J, j, slice(j, j + 1))

            def attn_rsqrt(k, j):
                rstd(lna_ve, lna_rstd, vea, rsa, k, J, j, slice(j, j + 1))

            def add_residual(k, j):
                need(pool, rn_ready, passed(k, J, j))
                need(pool, xr_ld[j], passed(k, 16, 15))
                need(pool, ob_ready, passed(back(k, 2), J, j))
                nc.gpsimd.tensor_tensor(x1[k[1]][:, j], XR[j][:, 0, :], r[j][:], ALU.add).then_inc(x1_ready, 1)

            def ln2_rsqrt(k, j):
                rstd(ln2_ve, ln2_rstd, ve2, rs2, k, J, j, slice(j, j + 1))

            def hidden_lo(k, q):
                need(pool, hh_ready, passed(k, 4, q))
                nc.gpsimd.tensor_tensor(hl[:, 2 * q:2 * q + 2, :], hf[q % 2][:],
                                        hh[:, 2 * q:2 * q + 2, :].bitcast(F32),
                                        ALU.subtract).then_inc(hl_ready, 1)

            def ffn_rsqrt(k, j):
                rstd(lnf_ve, lnf_rstd, vef, rsf, k, J, j, slice(j, j + 1))

            def add_ffn(k, j):
                need(pool, fn_ready, passed(k, J, j))
                need(pool, out_st[j], passed(back(k, 1), 16, 15))
                nc.gpsimd.tensor_tensor(ob[j][:], x1[k[1]][:, j], ffo[j][:], ALU.add).then_inc(ob_ready, 1)

            run(pool, {"ln1 rsqrt": ln1_rsqrt, "mask": mask, "x for state": x_for_state, "skip": skip_term,
                       "mix": mix, "add inter": add_inter, "gate rsqrt": gate_rsqrt, "attn rsqrt": attn_rsqrt,
                       "add residual": add_residual, "ln2 rsqrt": ln2_rsqrt, "hidden lo": hidden_lo,
                       "ffn rsqrt": ffn_rsqrt, "add ffn": add_ffn})

        @block.vector
        def _(dve):
            dve.wait_ge(w_ld["win"], 16)
            nc.vector.tensor_copy(win_hi[:], win_f[:]).then_inc(prep, 1)
            dve.wait_ge(prep, 1)
            nc.vector.tensor_tensor(win_lo[:], win_f[:], win_hi[:].bitcast(F32), ALU.subtract).then_inc(prep, 1)
            dve.wait_ge(prep, 2)
            dve.wait_ge(consts, CONSTS)
            nc.vector.tensor_copy(wdt[:, :, 0:NH], win_hi[:, :, DIN - NH:DIN].bitcast(F32)).then_inc(prep, 1)
            nc.vector.tensor_copy(wdt[:, :, NH:2 * NH], win_lo[:, :, DIN - NH:DIN].bitcast(F32)).then_inc(prep, 1)
            dve.wait_ge(prep, 4)
            nc.vector.memset(sp[:], 0.0).then_inc(ready["win"], 1)

            def prepare_wout():
                dve.wait_ge(w_ld["wout"], 16)
                dve.wait_ge(w_ld["small"], 16 * 8)
                for c in range(KI):
                    nc.vector.tensor_scalar(wout_f[:, c, :], wout_f[:, c, :], nws[:, c:c + 1], None,
                                            ALU.mult).then_inc(prep, 1)
                dve.wait_ge(prep, 4 + KI)
                nc.vector.tensor_copy(wout_hi[:], wout_f).then_inc(prep, 1)
                dve.wait_ge(prep, 5 + KI)
                nc.vector.tensor_tensor(wout_lo[:], wout_f, wout_hi[:].bitcast(F32),
                                        ALU.subtract).then_inc(ready["wout"], 1)

            def ternary(n, wf, wt, done):
                nc.vector.tensor_scalar(wt[:], wf, nthr[:, n:n + 1], 1.0, ALU.is_ge, ALU.subtract).then_inc(prep, 1)
                dve.wait_ge(prep, 9 + KI + 4 * n)
                nc.vector.scalar_tensor_tensor(wt[:], wf, thr[:, n:n + 1], wt[:].bitcast(F32), ALU.is_gt,
                                               ALU.add).then_inc(done, 1)

            def prepare_w1():
                dve.wait_ge(absum_ps, 1)
                nc.vector.tensor_scalar(thr[:], pG[:, 0:2], 1.0 / (DM * FF), 1e-8, ALU.mult, ALU.max).then_inc(prep, 1)
                dve.wait_ge(prep, 6 + KI)
                nc.vector.tensor_scalar(nthr[:], thr[:], -0.5, None, ALU.mult).then_inc(prep, 1)
                nc.vector.tensor_scalar(thr[:], thr[:], 0.5, None, ALU.mult).then_inc(prep, 1)
                dve.wait_ge(prep, 8 + KI)
                ternary(0, w1_f, w1_t, ready["w1"])

            def prepare_w2():
                nc.vector.tensor_copy(b2r[0:1, :], b2s[0:1, :]).then_inc(prep, 1)
                nc.vector.tensor_copy(b2r[32:33, :], b2s[32:33, :]).then_inc(prep, 1)
                dve.wait_ge(prep, 11 + KI)
                nc.vector.tensor_tensor(b2r[32:33, :], b2s[32:33, :], b2r[32:33, :].bitcast(F32),
                                        ALU.subtract).then_inc(prep, 1)
                dve.wait_ge(prep, 12 + KI)
                ternary(1, w2_f, w2_t, ready["w2"])

            def stats(st, src, mv, s_mv, j):
                nc.vector.bn_stats(st[:, j, :], src)
                dve.drain()
                nc.vector.bn_aggr(mv[:, j, :], st[:, j, :]).then_inc(s_mv, 1)

            def add_eps(mv, ve, s_mv, s_ve, k, j):
                dve.wait_ge(s_mv, passed(k, J, j))
                nc.vector.tensor_scalar(ve[:, j:j + 1], mv[:, j, 1:2], EPS, None, ALU.add).then_inc(s_ve, 1)

            def normalize(dst, src, mv, rs, j, done):
                nc.vector.tensor_scalar(dst, src, mv[:, j, 0:1], rs[:, j:j + 1], ALU.subtract,
                                        ALU.mult).then_inc(done, 1)

            def by_head(ap):
                return ap.rearrange("p (h d) -> p h d", h=NH)

            def per_head(ap):
                return ap.unsqueeze(2).to_broadcast([P, NH, HD])

            def ln1_stats(k, _):
                dve.wait_ge(x_ld[k[1]], 16 * (k[0] + 1))
                for j in range(J):
                    nc.vector.bn_stats(st1[:, j, :], XU[k[1]][:, j, 0, :])
                for j in range(J):
                    if j == 0:
                        dve.drain()
                    nc.vector.bn_aggr(mv1[:, j, :], st1[:, j, :]).then_inc(ln1_mv, 1)

            def ln1_eps(k, _):
                dve.wait_ge(ln1_mv, passed(k, J, J - 1))
                nc.vector.tensor_scalar(ve1[:], mv1[:, :, 1], EPS, None, ALU.add).then_inc(ln1_ve, 1)

            def u(k, _):
                need(dve, ln1_rstd, passed(k, 1, 0))
                for j in range(J):
                    normalize(XU[k[1]][:, j, 1, :], XU[k[1]][:, j, 0, :], mv1, rs1, j, u_ready)

            def u_lo(k, _):
                s = k[1]
                need(dve, uTh_ready, passed(k, 1, 0))
                if s == 1:
                    need(dve, uTl_ready, passed(back(k, 1), 1, 0))
                    nc.vector.tensor_copy(uTl[1][:, :, 0:CARRY], uTl[0][:, :, UW - CARRY:UW].bitcast(F32))
                nc.vector.tensor_tensor(uTl[s][:, :, CARRY:UW],
                                        pA[0][:].rearrange("p (c t) -> p c t", c=KM),
                                        uTh[s][:, :, CARRY:UW].bitcast(F32),
                                        ALU.subtract).then_inc(uTl_ready, 1)
                if is_half(k, 0):
                    prepare_wout()

            def conv(k, q):
                for tap in range(1, TAPS):
                    for c in range(2):
                        m = 2 * q + c
                        if tap == 1:
                            need(dve, conv_first, passed(k, CH, m))
                        else:
                            dve.wait_ge(conv_tap, passed(k, 2 * CH, 4 * q + 2 * (tap - 2) + c))
                        w = TAPS - 1 - tap
                        nc.vector.scalar_tensor_tensor(
                            acc[q % 2][:, c, :], pA[c][:, 1 + w:1 + w + HALF], convw[:, m, w:w + 1],
                            acc[q % 2][:, c, :], ALU.mult, ALU.add
                        ).then_inc(conv_done if tap == TAPS - 1 else conv_tap, 1)
                if is_half(k, 0) and q < 2:
                    (prepare_w1, prepare_w2)[q]()

            def sp_did(k, i):
                dve.wait_ge(sp_step, passed(k, SP_STEPS, i))

            def softplus(k, n):
                v, a, e, d, rc, z, qq, p = (sp[:, i] for i in range(8))
                if n not in (0, 3, 13):
                    sp_did(k, n - 1)

                if n == 0:
                    need(dve, dtt_ready, passed(k, 1, 0))
                    op = nc.vector.tensor_tensor(v, dtt[:, :, 0:NH], dtt[:, :, NH:2 * NH], ALU.add)
                elif n == 1:
                    op = nc.vector.tensor_tensor(v, v, dtb[:].unsqueeze(1).to_broadcast([P, J, NH]), ALU.add)
                elif n == 2:
                    op = nc.vector.scalar_tensor_tensor(a, v, -1.0, v, ALU.mult, ALU.max)
                elif n == 3:
                    need(dve, sp_exp, passed(k, 1, 0))
                    op = nc.vector.tensor_scalar(d, e, 2.0, None, ALU.add)
                elif n == 4:
                    op = nc.vector.reciprocal(rc, d)
                elif n == 5:
                    op = nc.vector.tensor_tensor(z, e, rc, ALU.mult)
                elif n == 6:
                    op = nc.vector.tensor_tensor(qq, z, z, ALU.mult)
                elif n == 7:
                    op = nc.vector.tensor_scalar(p, qq, 1.0 / 11, None, ALU.mult)
                elif n < 12:
                    op = nc.vector.scalar_tensor_tensor(p, p, 1.0 / (25 - 2 * n), qq, ALU.add, ALU.mult)
                elif n == 12:
                    op = nc.vector.scalar_tensor_tensor(p, p, 1.0, z, ALU.add, ALU.mult)
                elif n == 13:
                    op = nc.vector.tensor_scalar(d, v, 0.0, None, ALU.max)
                elif n == 14:
                    if is_half(k, 0):
                        dve.wait_ge(a_exp, 1)
                    op = nc.vector.scalar_tensor_tensor(dts[k[1]][:], p, 2.0, d, ALU.mult, ALU.add)
                else:
                    op = nc.vector.tensor_tensor(dA[:, 0:J * NH].rearrange("p (j h) -> p j h", j=J), dts[k[1]][:],
                                                 a_pos[:].unsqueeze(1).to_broadcast([P, J, NH]), ALU.mult)
                op.then_inc(sp_step if n < SP_STEPS else dA_ready, 1)

            def dt_decay(k, _):
                s = k[1]
                need(dve, ecum_ready, passed(k, 1, 0))
                nc.vector.tensor_tensor(etot[s][:], ecum[s][:, 0], ecum[s][:, 1], ALU.mult).then_inc(etot_ready, 1)
                nc.vector.tensor_tensor(dtdec[s][:], dts[s][:], ecum[s][:, 1], ALU.mult).then_inc(dtdec_ready, 1)

            def x_dt(k, j):
                need(dve, xtok_ready, passed(k, J, j))
                need(dve, intra_ps, passed(back(k, 1), J, j))
                nc.vector.tensor_tensor(by_head(xdt[j][:]), by_head(xtok[j][:]), per_head(dts[k[1]][:, j, :]),
                                        ALU.mult).then_inc(xdt_ready, 1)

            def inter(k, j):
                if not first_tile(k, j):
                    need(dve, inter_ps, inter_count(k, j))
                    nc.vector.tensor_tensor(by_head(t1[j][:]), by_head(pY[:]), per_head(ecum[k[1]][:, 0, j, :]),
                                            ALU.mult).then_inc(t1_ready, 1)

            def y(k, j):
                need(dve, intra_ps, passed(k, J, j))
                if first_tile(k, j):
                    need(dve, xd_ready, passed(k, J, j))
                else:
                    need(dve, yx_ready, inter_count(k, j))
                nc.vector.tensor_tensor(t1[j][:], pY[:], xd[j][:], ALU.add).then_inc(y_ready, 1)

            def gate(k, j):
                dve.wait_ge(y_ready, passed(k, J, j))
                need(dve, sz_ready, passed(k, J, j))
                nc.vector.tensor_tensor(g[j][:], t1[j][:], sz[k[1]][:, j, :], ALU.mult).then_inc(g_ready, 1)

            def gate_mean(k, j):
                need(dve, ss_ready, passed(k, J, j))
                nc.vector.tensor_scalar(vg[:, j:j + 1], ss[:, j:j + 1], 1.0 / DI, EPS, ALU.mult,
                                        ALU.add).then_inc(vg_ready, 1)

            def gate_lo(k, j):
                need(dve, gTh_ready, passed(k, J, j))
                nc.vector.tensor_tensor(gTl[j][:], pT[:].rearrange("p (c t) -> p c t", c=KI), gTh[j][:].bitcast(F32),
                                        ALU.subtract).then_inc(gTl_ready, 1)

            def attn_out(k, j):
                need(dve, proj_ps, passed(k, J, j))
                need(dve, rg_ready, passed(k, J, j))
                dve.wait_ge(xr_ld[j], passed(k, 16, 15))
                nc.vector.scalar_tensor_tensor(r[j][:], pS[:, 0:DM], rg[:, j:j + 1], XR[j][:, 1, :], ALU.mult,
                                               ALU.add).then_inc(r_ready, 1)

            def attn_stats(k, j):
                dve.wait_ge(r_ready, passed(k, J, j))
                stats(sta, r[j][:], mva, lna_mv, j)

            def attn_eps(k, j):
                add_eps(mva, vea, lna_mv, lna_ve, k, j)

            def attn_norm(k, j):
                need(dve, lna_rstd, passed(k, J, j))
                normalize(r[j][:], r[j][:], mva, rsa, j, rn_ready)

            def scale_state(k, j):
                if not last_tile(k, j) and not first_tile(k, j):
                    need(dve, inter_ps, inter_count(k, j))
                    need(dve, s_ready, state_count(k, j) + -1)
                    need(dve, etot_ready, passed(k, 1, 0))
                    nc.vector.tensor_tensor(by_head(S[:]), by_head(S[:]), per_head(etot[k[1]][:, j, :]),
                                            ALU.mult).then_inc(s_scaled, 1)

            def new_state(k, j):
                b, s = k
                if last_tile(k, j):
                    return
                need(dve, state_ps, state_count(k, j))
                if first_tile(k, j):
                    need(dve, inter_ps, 3 * b)
                    nc.vector.tensor_copy(S[:], pS[:]).then_inc(s_ready, 1)
                else:
                    dve.wait_ge(s_scaled, 2 * b + 2 * s + j)
                    nc.vector.tensor_tensor(S[:], pS[:], S[:], ALU.add).then_inc(s_ready, 1)

            def ln2_stats(k, j):
                need(dve, x1_ready, passed(k, J, j))
                stats(st2, x1[k[1]][:, j, :], mv2, ln2_mv, j)

            def ln2_eps(k, j):
                add_eps(mv2, ve2, ln2_mv, ln2_ve, k, j)

            def u2_norm(k, j):
                need(dve, ln2_rstd, passed(k, J, j))
                normalize(u2[j][:], x1[k[1]][:, j, :], mv2, rs2, j, u2_ready)

            def u2_lo(k, j):
                need(dve, u2Th_ready, passed(k, J, j))
                cols = slice(j * P, (j + 1) * P)
                nc.vector.tensor_tensor(u2Tl[k[1]][:, :, cols], pG[:, 0:DM].rearrange("p (c t) -> p c t", c=KM),
                                        u2Th[k[1]][:, :, cols].bitcast(F32), ALU.subtract).then_inc(u2Tl_ready, 1)

            def ffn_stats(k, j):
                need(dve, down_ps, passed(k, J, j))
                stats(stf, pF[j][:, 0:DM], mvf, lnf_mv, j)

            def ffn_eps(k, j):
                add_eps(mvf, vef, lnf_mv, lnf_ve, k, j)

            def ffn_norm(k, j):
                need(dve, lnf_rstd, passed(k, J, j))
                need(dve, ob_ready, passed(back(k, 1), J, j))
                normalize(ffo[j][:], pF[j][:, 0:DM], mvf, rsf, j, fn_ready)

            run(dve, {"ln1 stats": ln1_stats, "ln1 eps": ln1_eps, "attn eps": attn_eps, "ln2 eps": ln2_eps,
                      "ffn eps": ffn_eps, "u": u, "u lo": u_lo, "conv taps": conv,
                      "softplus": softplus, "dt decay": dt_decay,
                      "x dt": x_dt, "inter decay": inter, "y": y, "gate": gate, "gate mean": gate_mean,
                      "gate lo": gate_lo, "attn out": attn_out, "attn stats": attn_stats,
                      "attn norm": attn_norm, "scale state": scale_state, "new state": new_state,
                      "ln2 stats": ln2_stats, "u2": u2_norm, "u2 lo": u2_lo, "ffn stats": ffn_stats,
                      "ffn norm": ffn_norm})

        @block.scalar
        def _(act):
            act.dma_start(convw[:], conv_w).then_inc(w_ld["small"], 16)
            act.dma_start(convb[:], conv_b).then_inc(w_ld["small"], 16)
            act.dma_start(b1s[:], b1).then_inc(w_ld["small"], 16)
            act.dma_start(nws[:], norm_w).then_inc(w_ld["small"], 16)
            for dst, src in ((b2s, b2), (dtb, dt_bias), (a_pos, a_log), (dsk, d_skip)):
                act.dma_start(dst[:], src.partition_broadcast(P)).then_inc(w_ld["small"], 16)
            act.dma_start(w1_f.rearrange("p (c n) -> p c n", c=KM),
                          w1.rearrange("(c p) n -> p c n", p=P)).then_inc(w_ld["w1"], 16)
            act.dma_start(w2_f.rearrange("p (c n) -> p c n", c=KF),
                          w2.rearrange("(c p) n -> p c n", p=P)).then_inc(w_ld["w2"], 16)
            act.dma_start(wout_f, w_out.rearrange("(c p) n -> p c n", p=P)).then_inc(w_ld["wout"], 16)
            act.wait_ge(w_ld["small"], 16 * 8)
            nc.scalar.activation(a_pos[:], a_pos[:], ACT.Exp).then_inc(a_exp, 1)
            act.wait_ge(consts, CONSTS)
            for n, (name, wf) in enumerate((("w1", w1_f), ("w2", w2_f))):
                act.wait_ge(w_ld[name], 16)
                act.wait_ge(absum_ready, n)
                nc.scalar.activation(hl[:].rearrange("p k t -> p (k t)"), wf, ACT.Abs,
                                     accum_out=absum[:, n:n + 1]).then_inc(absum_ready, 1)

            def uT_hi(k, _):
                s = k[1]
                need(act, uT_ps, passed(k, 1, 0))
                need(act, conv_ps, passed(back(k, 2), CH, CH - 1))
                if s == 1:
                    need(act, uTh_ready, passed(back(k, 1), 1, 0))
                    nc.scalar.copy(uTh[1][:, :, 0:CARRY], uTh[0][:, :, UW - CARRY:UW].bitcast(F32))
                nc.scalar.copy(uTh[s][:, :, CARRY:UW],
                               pA[0][:].rearrange("p (c t) -> p c t", c=KM)).then_inc(uTh_ready, 1)

            def dt_out(k, _):
                need(act, dt_ps, passed(k, 1, 0))
                need(act, dtT_ps, passed(back(k, 1), 1, 0))
                nc.scalar.copy(dtr[:], pA[1][:, 0:HALF]).then_inc(dtr_ready, 1)

            def conv_first_tap(k, q):
                need(act, xbc_ready, passed(k, 3, 0) if q == 2 else passed(back(k, 1), 3, 2 if q == 0 else 1))
                for c in range(2):
                    m = 2 * q + c
                    need(act, conv_ps, passed(k, CH, m))
                    nc.scalar.activation(acc[q % 2][:, c, :], pA[c][:, CARRY:UW], ACT.Identity,
                                         bias=convb[:, m:m + 1], scale=convw[:, m, TAPS - 1:TAPS]).then_inc(conv_first, 1)

            def silu(k, q):
                need(act, conv_done, passed(k, CH, 2 * q + 1))
                if is_half(k, 0):
                    act.wait_ge(ready["wout"], 1)
                need(act, intra_ps, passed(back(k, 2), J, J - 1))
                nc.scalar.activation(xbc[k[1]][:, 2 * q:2 * q + 2, :], acc[q % 2][:], ACT.Silu).then_inc(xbc_ready, 1)

            def dt_token(k, _):
                need(act, dtT_ps, passed(k, 1, 0))
                need(act, sp_step, passed(back(k, 1), SP_STEPS, 0))
                nc.scalar.copy(dtt[:], pA[0][:, 0:J * P].rearrange("p (j n) -> p j n", j=J)[:, :, 0:2 * NH]
                               ).then_inc(dtt_ready, 1)

            def softplus_exp(k, _):
                need(act, sp_step, passed(k, SP_STEPS, 2))
                nc.scalar.activation(sp[:, 2], sp[:, 1], ACT.Exp, scale=-1.0).then_inc(sp_exp, 1)

            def sums_head(k, _):
                need(act, cum_ps, passed(k, 1, 0))
                need(act, cum_st, passed(back(k, 1), 16, 15))
                need(act, cumT_ps, passed(back(k, 1), 1, 0))
                nc.scalar.copy(cr[:].rearrange("p a i -> p (a i)"), pA[0][:, 0:2 * P]).then_inc(cr_ready, 1)

            def sums_token(k, _):
                n = J * NH
                need(act, cumT_ps, passed(k, 1, 0))
                nc.scalar.mul(cum[k[1]][:].rearrange("p j h -> p (j h)"), pA[0][:, 0:n], -1.0).then_inc(cum_ready, 1)
                nc.scalar.activation(ecum[k[1]][:].rearrange("p a j h -> p a (j h)"),
                                     pA[0][:, 0:2 * P].rearrange("p (a i) -> p a i", a=2)[:, :, 0:n],
                                     ACT.Exp, scale=-1.0).then_inc(ecum_ready, 1)

            def z_silu(k, j):
                need(act, z_ps, passed(k, J, j))
                need(act, g_ready, passed(back(k, 2), J, j))
                nc.scalar.activation(sz[k[1]][:, j, :], pA[1][:], ACT.Silu).then_inc(sz_ready, 1)

            def x_token(k, j):
                before = passed(back(k, 1), J, j)
                need(act, xT_ps, passed(k, J, j))
                need(act, xdt_ready, before)
                need(act, xd_ready, before)
                nc.scalar.copy(xtok[j][:], pT[:]).then_inc(xtok_ready, 1)

            def b_and_g(k, j):
                s = k[1]
                need(act, g_ps, passed(k, J, j))
                need(act, gm_ready, passed(back(k, 1), J, j))
                need(act, state_ps, 3 * k[0] + (-1 if (s, j) == (0, 1) else s + j))
                nc.scalar.copy(bg[j][:].rearrange("p a t -> p (a t)"), pG[:, 0:2 * P]).then_inc(bg_ready, 1)

            def decay(k, j):
                s = k[1]
                act.wait_ge(r_ld[s], 16 * (k[0] + 1))
                act.wait_ge(cum_ready, passed(k, 1, 0))
                for h in range(NH):
                    last = nc.scalar.activation(R[s][:, j, h, :], R[s][:, j, h, :], ACT.Relu,
                                                bias=cum[s][:, j, h:h + 1])
                last.then_inc(diff_ready, 1)

            def decay_exp(k, j):
                act.wait_ge(diff_ready, passed(k, J, j))
                nc.scalar.activation(R[k[1]][:, j], R[k[1]][:, j], ACT.Exp, scale=-1.0).then_inc(exp_ready, 1)

            def gate_square(k, j):
                need(act, g_ready, passed(k, J, j))
                need(act, ss_ready, passed(k, J, j + -1))
                nc.scalar.activation(sqj[:], g[j][:], ACT.Square, accum_out=ss[:, j:j + 1]).then_inc(ss_ready, 1)

            def gate_hi(k, j):
                need(act, gT_ps, passed(k, J, j))
                need(act, proj_ps, passed(back(k, 1), J, j))
                nc.scalar.copy(gTh[j][:], pT[:].rearrange("p (c t) -> p c t", c=KI)).then_inc(gTh_ready, 1)

            def u2_hi(k, j):
                need(act, u2T_ps, passed(k, J, j))
                need(act, up_ps, passed(back(k, 2), 4, 3))
                nc.scalar.copy(u2Th[k[1]][:, :, j * P:(j + 1) * P],
                               pG[:, 0:DM].rearrange("p (c t) -> p c t", c=KM)).then_inc(u2Th_ready, 1)

            def gelu(k, q):
                need(act, up_ps, passed(k, 4, q))
                need(act, hl_ready, passed(k if q >= 2 else back(k, 1), 4, (q + 2) % 4))
                for c in range(2):
                    nc.scalar.activation(hf[q % 2][:, c, :], pF[q % 2][:, c * HALF:(c + 1) * HALF], ACT.Gelu,
                                         bias=b1s[:, 2 * q + c:2 * q + c + 1]).then_inc(gelu_ready, 1)

            def hidden_hi(k, q):
                act.wait_ge(gelu_ready, passed(k, KF, 2 * q + 1))
                need(act, down_ps, passed(back(k, 1), J, J - 1))
                nc.scalar.copy(hh[:, 2 * q:2 * q + 2, :], hf[q % 2][:]).then_inc(hh_ready, 1)

            run(act, {"u hi": uT_hi, "dt rows": dt_out, "conv first": conv_first_tap, "conv silu": silu,
                      "dt token": dt_token, "softplus exp": softplus_exp, "sums head": sums_head,
                      "sums token": sums_token, "z silu": z_silu, "x token": x_token, "B and G": b_and_g,
                      "decay": decay, "decay exp": decay_exp, "gate square": gate_square, "gate hi": gate_hi,
                      "u2 hi": u2_hi,
                      "gelu": gelu, "hidden hi": hidden_hi})

        @block.tensor
        def _(pe):
            pe.wait_ge(absum_ready, 2)
            pe.wait_ge(consts, CONSTS)
            nc.tensor.matmul(pG[:, 0:2], ones[:], absum[:], start=True, stop=True).then_inc(absum_ps, 1)
            pe.wait_ge(ready["win"], 1)

            def transpose(dst, src):
                return nc.tensor.matmul(dst, src, ident[:], is_transpose=True, start=True, stop=True)

            def uT(k, _):
                s = k[1]
                need(pe, u_ready, passed(k, J, J - 1))
                need(pe, conv_done, passed(back(k, 1), CH, 4))
                for c in range(KM):
                    for j in range(J):
                        last = transpose(pA[0][:, c * HALF + j * P:c * HALF + (j + 1) * P],
                                         XU[s][:, j, 1, c * P:(c + 1) * P])
                last.then_inc(uT_ps, 1)

            def dt(k, _):
                s = k[1]
                need(pe, uTl_ready, passed(k, 1, 0))
                need(pe, conv_done, passed(back(k, 1), CH, 5))
                for c in range(KM):
                    for n, uT_part in enumerate((uTh, uTl)):
                        last = nc.tensor.matmul(pA[1][:, 0:HALF], wdt[:, c, :], uT_part[s][:, c, CARRY:UW],
                                                start=(c, n) == (0, 0), stop=(c, n) == (KM - 1, 1))
                last.then_inc(dt_ps, 1)

            def conv_in(k, q):
                s = k[1]
                for i in range(2):
                    m = 2 * q + i
                    if i == 0:
                        need(pe, (uTl_ready, dtt_ready, ecum_ready)[q], passed(k, 1, 0))
                    elif q == 0:
                        need(pe, dtr_ready, passed(k, 1, 0))
                    else:
                        need(pe, sz_ready, passed(k, J, q - 1))
                    cols = slice(DI + m * P, DI + (m + 1) * P)
                    for c in range(KM):
                        for n, (w, uT_part) in enumerate(((win_hi, uTh), (win_hi, uTl), (win_lo, uTh))):
                            last = nc.tensor.matmul(pA[i][:, 0:UW], w[:, c, cols], uT_part[s][:, c, :],
                                                    start=(c, n) == (0, 0), stop=(c, n) == (KM - 1, 2))
                    last.then_inc(conv_ps, 1)

            def dtT(k, _):
                need(pe, dtr_ready, passed(k, 1, 0))
                need(pe, conv_done, passed(k, CH, 0))
                for j in range(J):
                    last = transpose(pA[0][:, j * P:(j + 1) * P], dtr[:, j * P:(j + 1) * P])
                last.then_inc(dtT_ps, 1)

            def sums(k, _):
                need(pe, dA_ready, passed(k, 1, 0))
                need(pe, conv_done, passed(k, CH, 2))
                nc.tensor.matmul(pA[0][:, 0:2 * P], dA[:], tri[:].rearrange("p a i -> p (a i)"),
                                 start=True, stop=True).then_inc(cum_ps, 1)

            def sumsT(k, _):
                need(pe, cr_ready, passed(k, 1, 0))
                for a in range(2):
                    last = transpose(pA[0][:, a * P:(a + 1) * P], cr[:, a, :])
                last.then_inc(cumT_ps, 1)

            def z(k, j):
                s = k[1]
                need(pe, conv_done, passed(k, CH, 2 * j + 1))
                for c in range(KM):
                    for n, (uT_part, w) in enumerate(((uTh, win_hi), (uTh, win_lo), (uTl, win_hi))):
                        last = nc.tensor.matmul(pA[1][:], uT_part[s][:, c, CARRY + j * P:CARRY + (j + 1) * P],
                                                w[:, c, 0:DI], start=(c, n) == (0, 0), stop=(c, n) == (KM - 1, 2))
                last.then_inc(z_ps, 1)

            def x_and_g(k, j):
                s = k[1]
                cols = slice(j * P, (j + 1) * P)
                need(pe, xbc_ready, passed(k, 3, 2))
                if j == 0:
                    need(pe, gTl_ready, passed(back(k, 1), J, 1))
                else:
                    need(pe, xtok_ready, passed(k, J, 0))
                for m in range(XS):
                    last = transpose(pT[:, m * P:(m + 1) * P], xbc[s][:, m, cols])
                last.then_inc(xT_ps, 1)
                if j == 1:
                    need(pe, bg_ready, passed(k, J, 0))
                need(pe, u2Tl_ready, passed(back(k, 1), J, j))
                transpose(pG[:, 0:P], xbc[s][:, XS, cols])
                nc.tensor.matmul(pG[:, P:2 * P], xbc[s][:, XS, cols], xbc[s][:, XS + 1, cols],
                                 start=True, stop=True).then_inc(g_ps, 1)

            def tile_before(k, j):
                return passed(k if j else back(k, 1), J, 1 - j)

            def inter(k, j):
                if not first_tile(k, j):
                    need(pe, s_ready, state_count(k, j) + -1)
                    need(pe, y_ready, tile_before(k, j))
                    nc.tensor.matmul(pY[:], xbc[k[1]][:, XS + 1, j * P:(j + 1) * P], S[:],
                                     start=True, stop=True).then_inc(inter_ps, 1)

            def intra(k, j):
                s = k[1]
                if first_tile(k, j):
                    need(pe, y_ready, tile_before(k, j))
                else:
                    need(pe, t1_ready, inter_count(k, j))
                need(pe, mix_ready, passed(k, J, j))
                need(pe, xdt_ready, passed(k, J, j))
                for h in range(NH):
                    cols = slice(h * HD, (h + 1) * HD)
                    last = nc.tensor.matmul(pY[:, cols], R[s][:, j, h, :], xdt[j][:, cols],
                                            start=True, stop=True)
                last.then_inc(intra_ps, 1)

            def gateT(k, j):
                need(pe, g_ready, passed(k, J, j))
                if j == 0:
                    need(pe, xtok_ready, passed(k, J, 1))
                else:
                    need(pe, gTl_ready, passed(k, J, 0))
                for c in range(KI):
                    last = transpose(pT[:, c * P:(c + 1) * P], g[j][:, c * P:(c + 1) * P])
                last.then_inc(gT_ps, 1)

            def project(k, j):
                need(pe, gTl_ready, passed(k, J, j))
                if is_half(k, 0):
                    pe.wait_ge(ready["wout"], 1)
                if last_tile(k, j):
                    need(pe, r_ready, passed(k, J, 0))
                else:
                    need(pe, s_ready, state_count(k, j))
                for c in range(KI):
                    for n, (gT_part, w) in enumerate(((gTh, wout_hi), (gTh, wout_lo), (gTl, wout_hi))):
                        last = nc.tensor.matmul(pS[:, 0:DM], gT_part[j][:, c, :], w[:, c, :],
                                                start=(c, n) == (0, 0), stop=(c, n) == (KI - 1, 2))
                last.then_inc(proj_ps, 1)

            def state(k, j):
                if not last_tile(k, j):
                    need(pe, xst_ready, state_count(k, j))
                    need(pe, bg_ready, passed(k, J, j))
                    need(pe, r_ready, tile_before(k, j))
                    nc.tensor.matmul(pS[:], bg[j][:, 0, :], xst[j][:], start=True, stop=True).then_inc(state_ps, 1)

            def u2T(k, j):
                need(pe, u2_ready, passed(k, J, j))
                if j == 0 or is_half(k, 2 * B - 1):
                    need(pe, bg_ready, passed(k, J, 1))
                else:
                    need(pe, bg_ready, passed(back(k, -1), J, 0))
                if is_half(k, 2 * B - 1) and j == 1:
                    need(pe, u2Tl_ready, passed(k, J, 0))
                for c in range(KM):
                    last = transpose(pG[:, c * P:(c + 1) * P], u2[j][:, c * P:(c + 1) * P])
                last.then_inc(u2T_ps, 1)

            def up(k, q):
                s = k[1]
                need(pe, u2Tl_ready, passed(k, J, J - 1))
                if is_half(k, 0):
                    pe.wait_ge(ready["w1"], 1)
                if q < 2:
                    need(pe, fn_ready, passed(back(k, 1), J, q))
                else:
                    need(pe, gelu_ready, passed(k, KF, 2 * (q - 2) + 1))
                for i in range(2):
                    m = 2 * q + i
                    for c in range(KM):
                        for n, part in enumerate((u2Th, u2Tl)):
                            last = nc.tensor.matmul(pF[q % 2][:, i * HALF:(i + 1) * HALF],
                                                    w1_t[:, c * FF + m * P:c * FF + (m + 1) * P], part[s][:, c, :],
                                                    start=(c, n) == (0, 0), stop=(c, n) == (KM - 1, 1))
                last.then_inc(up_ps, 1)

            def down(k, j):
                need(pe, hl_ready, passed(k, 4, 3))
                need(pe, gelu_ready, passed(k, KF, 5 + 2 * j))
                if is_half(k, 0):
                    pe.wait_ge(ready["w2"], 1)
                nc.tensor.matmul(pF[j][:, 0:DM], ones_r[:], b2r[:], start=True, stop=False)
                for c in range(KF):
                    for n, part in enumerate((hh, hl)):
                        last = nc.tensor.matmul(pF[j][:, 0:DM], part[:, c, j * P:(j + 1) * P],
                                                w2_t[:, c * DM:(c + 1) * DM],
                                                start=False, stop=(c, n) == (KF - 1, 1))
                last.then_inc(down_ps, 1)

            run(pe, {"uT": uT, "dt": dt, "conv": conv_in, "dtT": dtT, "sums": sums, "sumsT": sumsT, "z": z,
                     "xT and G": x_and_g, "inter": inter, "intra": intra, "gateT": gateT,
                     "project": project, "state": state, "u2T": u2T, "up": up, "down": down})


def kernel(L0_attn_x, L0_attn_in_proj_w, L0_attn_conv_w, L0_attn_conv_b, L0_attn_dt_bias, L0_attn_A_log,
           L0_attn_D, L0_attn_norm_w, L0_attn_out_proj_w, L0_ffn_W1, L0_ffn_b1, L0_ffn_W2, L0_ffn_b2):
    import concourse.bacc as bacc
    from concourse.bass_utils import run_bass_kernel_spmd

    def by_partition(a):
        a = np.asarray(a)
        return np.moveaxis(a.reshape(a.shape[0] // P, P, *a.shape[1:]), 0, 1)

    arrays = {
        "x": L0_attn_x, "w_in": np.asarray(L0_attn_in_proj_w).T,
        "conv_w": by_partition(L0_attn_conv_w), "conv_b": by_partition(L0_attn_conv_b),
        "dt_bias": L0_attn_dt_bias, "a_log": L0_attn_A_log, "d_skip": L0_attn_D,
        "norm_w": by_partition(L0_attn_norm_w), "w_out": np.asarray(L0_attn_out_proj_w).T,
        "w1": np.asarray(L0_ffn_W1).T, "b1": by_partition(L0_ffn_b1),
        "w2": np.asarray(L0_ffn_W2).T, "b2": L0_ffn_b2,
    }
    arrays = {n: np.ascontiguousarray(a) for n, a in arrays.items()}
    nc = bacc.Bacc("TRN2", target_bir_lowering=False, num_devices=1)
    aps = [nc.dram_tensor(n, a.shape, mybir.dt.from_np(a.dtype), kind="ExternalInput").ap()
           for n, a in arrays.items()]
    heads = arrays["dt_bias"].shape[0]
    cum_dram = nc.dram_tensor("cum_dram", (2, 2 * heads, P), F32, kind="Internal").ap()
    out = nc.dram_tensor("out", arrays["x"].shape, F32, kind="ExternalOutput").ap()
    build(nc, *aps, cum_dram, out)
    r = run_bass_kernel_spmd(nc, [arrays], core_ids=[0])
    return r.results[0]["out"]
```
